# Optimizing a Trainium2 kernel written in Bass

```python
import numpy as np
import jax
import jax.numpy as jnp

def _softmax(x, axis=-1):
    return jax.nn.softmax(x, axis=axis)

def _gelu(x):
    return jax.nn.gelu(x, approximate=True)

def _silu(x):
    return jax.nn.silu(x)

def _sigmoid(x):
    return jax.nn.sigmoid(x)

def _layernorm(x, axis=-1, eps=1e-05):
    m = jnp.mean(x, axis=axis, keepdims=True)
    v = jnp.var(x, axis=axis, keepdims=True)
    return (x - m) / jnp.sqrt(v + eps)

def _scatter_add(tgt, idx, src, axis=0):
    return tgt.at[idx].add(src)

def _segment_sum(src, seg, n):
    return jax.ops.segment_sum(src, seg, n)
kernel_name = 'mk_cond_resid_d4_seqx_r4_6d897b'

def setup_inputs(seed: int=0):
    np.random.seed(seed)
    _w = jnp.asarray

    def _rec_inputs():
        import jax
        import jax.numpy as jnp
        _rk = jax.random.key(seed)
        x = 8.748e-05 + 1 * jax.random.normal(jax.random.fold_in(_rk, 1), (4, 512, 512), jnp.float32)
        _lenS = 512 - jax.random.randint(jax.random.fold_in(_rk, 7), (4,), 0, max(1, 512 // 4) + 1, jnp.int32)
        _lenS2 = 512 - jax.random.randint(jax.random.fold_in(_rk, 8), (4,), 0, max(1, 512 // 4) + 1, jnp.int32)
        fside_BxSx1_0 = -0.00499425 + 1.0058 * jax.random.normal(jax.random.fold_in(_rk, 11), (4, 512, 1), jnp.float32)
        cond_2048 = 0.00513981 + 1.0024 * jax.random.normal(jax.random.fold_in(_rk, 12), (4, 512), jnp.float32)
        return (x, fside_BxSx1_0, cond_2048)
    x, fside_BxSx1_0, cond_2048 = _rec_inputs()

    def _L0_cond_setup():
        import jax, jax.numpy as jnp
        import numpy as np
        G, N, K = (16, 512, 5120)
        key = jax.random.key(seed)
        k1, k2, k3 = jax.random.split(key, 3)
        return {'emb_s': jax.random.normal(k1, (G, N, 1), dtype=jnp.float32), 'emb_t': jax.random.normal(k2, (G, 1, N), dtype=jnp.float32), 'attention_weights': jax.random.normal(k3, (G, N, N), dtype=jnp.float32), 'k': K}
    _L0_cond_all = _L0_cond_setup()
    _L0_cond_in = {k: v for k, v in _L0_cond_all.items() if k in ()}
    del _L0_cond_all

    def _L1_cond_setup():
        import jax, jax.numpy as jnp
        import numpy as np
        HEADS = 16
        EPS = 1e-06

        def _rms_norm(x, g):
            xf = x.astype(jnp.float32)
            y = xf * jax.lax.rsqrt(jnp.mean(xf * xf, axis=-1, keepdims=True) + EPS)
            return y.astype(x.dtype) * g
        key = jax.random.key(seed)
        ks = jax.random.split(key, 6)
        b, n, dim, emb_dim = (4, 512, 512, 512)
        d_head = dim // HEADS
        return {'x': jax.random.normal(ks[0], (b, n, dim), jnp.float32), 'emb': jax.random.normal(ks[1], (b, 1, emb_dim), jnp.float32), 'W_emb': jax.random.normal(ks[2], (emb_dim, 2 * dim), jnp.float32) * emb_dim ** (-0.5), 'b_emb': jnp.zeros((2 * dim,), jnp.float32), 'g_norm': jnp.ones((dim,), jnp.float32), 'W_qkv': jax.random.normal(ks[3], (dim, 3 * dim), jnp.float32) * dim ** (-0.5), 'g_q': jnp.ones((d_head,), jnp.float32), 'g_k': jnp.ones((d_head,), jnp.float32), 'W_out': jax.random.normal(ks[4], (dim, dim), jnp.float32) * dim ** (-0.5)}
    _L1_cond_all = _L1_cond_setup()
    _L1_cond_in = {k: v for k, v in _L1_cond_all.items() if k in ('W_emb', 'b_emb', 'g_norm', 'W_qkv', 'g_q', 'g_k', 'W_out')}
    del _L1_cond_all

    def _L2_cond_setup():
        import jax, jax.numpy as jnp
        import numpy as np
        DT = 0.01
        EPSILON = 0.08
        ALPHA = 0.7
        BETA = 0.8
        CLAMP = 20.0
        B, T, N = (64, 128, 512)

        def _derivative(q, p, drive, coupling, bias):
            i_couple = jnp.tanh(q) @ coupling.T
            dq = q - q ** 3 / 3.0 - p + drive + i_couple + bias
            dp = EPSILON * (q + ALPHA - BETA * p)
            return (dq, dp)

        def _rk4_step(q, p, drive, coupling, bias):
            dq1, dp1 = _derivative(q, p, drive, coupling, bias)
            dq2, dp2 = _derivative(q + 0.5 * DT * dq1, p + 0.5 * DT * dp1, drive, coupling, bias)
            dq3, dp3 = _derivative(q + 0.5 * DT * dq2, p + 0.5 * DT * dp2, drive, coupling, bias)
            dq4, dp4 = _derivative(q + DT * dq3, p + DT * dp3, drive, coupling, bias)
            q_next = q + DT / 6.0 * (dq1 + 2 * dq2 + 2 * dq3 + dq4)
            p_next = p + DT / 6.0 * (dp1 + 2 * dp2 + 2 * dp3 + dp4)
            q_next = jnp.clip(q_next, -CLAMP, CLAMP)
            p_next = jnp.clip(p_next, -CLAMP, CLAMP)
            return (q_next, p_next)
        key = jax.random.key(seed)
        k1, k2, k3, k4 = jax.random.split(key, 4)
        return {'q0': jax.random.normal(k1, (B, N), dtype=jnp.float32), 'p0': jax.random.normal(k2, (B, N), dtype=jnp.float32), 'input_drive_seq': jax.random.normal(k3, (B, T, N), dtype=jnp.float32), 'coupling': jax.random.normal(k4, (N, N), dtype=jnp.float32) * 0.01, 'bias': jnp.zeros((N,), dtype=jnp.float32)}
    _L2_cond_all = _L2_cond_setup()
    _L2_cond_in = {k: v for k, v in _L2_cond_all.items() if k in ('coupling', 'bias')}
    del _L2_cond_all

    def _L3_cond_setup():
        import jax, jax.numpy as jnp
        import numpy as np
        B, T, D = (16, 128, 512)
        key = jax.random.key(seed)
        k0, k1, k2, k3 = jax.random.split(key, 4)
        scale = 1.0 / np.sqrt(D)
        return {'initial_state': jax.random.normal(k0, (B, D), jnp.float32), 'inputs': jax.random.normal(k1, (B, T, D), jnp.float32), 'W_ih': jax.random.normal(k2, (D, 3 * D), jnp.float32) * scale, 'W_hh': jax.random.normal(k3, (D, 3 * D), jnp.float32) * scale, 'b_ih': jnp.zeros((3 * D,), jnp.float32), 'b_hh': jnp.zeros((3 * D,), jnp.float32)}
    _L3_cond_all = _L3_cond_setup()
    _L3_cond_in = {k: v for k, v in _L3_cond_all.items() if k in ('W_ih', 'W_hh', 'b_ih', 'b_hh')}
    del _L3_cond_all
    return {'x': x, 'fside_BxSx1_0': fside_BxSx1_0, 'cond_2048': cond_2048, 'L1_cond_W_emb': _L1_cond_in['W_emb'], 'L1_cond_b_emb': _L1_cond_in['b_emb'], 'L1_cond_g_norm': _L1_cond_in['g_norm'], 'L1_cond_W_qkv': _L1_cond_in['W_qkv'], 'L1_cond_g_q': _L1_cond_in['g_q'], 'L1_cond_g_k': _L1_cond_in['g_k'], 'L1_cond_W_out': _L1_cond_in['W_out'], 'L2_cond_coupling': _L2_cond_in['coupling'], 'L2_cond_bias': _L2_cond_in['bias'], 'L3_cond_W_ih': _L3_cond_in['W_ih'], 'L3_cond_W_hh': _L3_cond_in['W_hh'], 'L3_cond_b_ih': _L3_cond_in['b_ih'], 'L3_cond_b_hh': _L3_cond_in['b_hh']}

def reference(x, fside_BxSx1_0, cond_2048, L1_cond_W_emb, L1_cond_b_emb, L1_cond_g_norm, L1_cond_W_qkv, L1_cond_g_q, L1_cond_g_k, L1_cond_W_out, L2_cond_coupling, L2_cond_bias, L3_cond_W_ih, L3_cond_W_hh, L3_cond_b_ih, L3_cond_b_hh):
    import jax
    import jax.numpy as jnp

    def _L0_cond_ref(emb_s, emb_t, attention_weights, k):
        import jax, jax.numpy as jnp
        import numpy as np
        G, N, K = (16, 512, 5120)
        g, n = (emb_s.shape[0], emb_s.shape[1])
        adj = emb_s * emb_t
        att = jax.nn.softmax(attention_weights, axis=-1) * (1.0 / np.sqrt(n).astype(np.float32))
        adj = adj * att
        diag = jnp.arange(n)
        adj = adj.at[:, diag, diag].set(-jnp.inf)
        flat = adj.reshape(g, n * n)
        _, idx = jax.lax.top_k(flat, k)
        rows = jnp.arange(g)[:, None]
        out = jnp.zeros((g, n * n), dtype=adj.dtype).at[rows, idx].set(1.0)
        return out.reshape(g, n, n)

    def _L1_cond_ref(x, emb, W_emb, b_emb, g_norm, W_qkv, g_q, g_k, W_out):
        import jax, jax.numpy as jnp
        import numpy as np
        HEADS = 16
        EPS = 1e-06

        def _rms_norm(x, g):
            xf = x.astype(jnp.float32)
            y = xf * jax.lax.rsqrt(jnp.mean(xf * xf, axis=-1, keepdims=True) + EPS)
            return y.astype(x.dtype) * g
        b, n, dim = x.shape
        h = HEADS
        d = dim // h
        scale_shift = emb @ W_emb + b_emb
        scale, shift = jnp.split(scale_shift, 2, axis=-1)
        xn = _rms_norm(x, g_norm) * (1.0 + scale) + shift
        qkv = xn @ W_qkv
        qkv = qkv.reshape(b, n, 3, h, d)
        q, k, v = jnp.moveaxis(qkv, 2, 0)
        q = jnp.swapaxes(q, 1, 2)
        k = jnp.swapaxes(k, 1, 2)
        v = jnp.swapaxes(v, 1, 2)
        q = _rms_norm(q, g_q)
        k = _rms_norm(k, g_k)
        logits = jnp.einsum('bhqd,bhkd->bhqk', q, k) * d ** (-0.5)
        attn = jax.nn.softmax(logits, axis=-1)
        o = jnp.einsum('bhqk,bhkd->bhqd', attn, v)
        o = jnp.swapaxes(o, 1, 2).reshape(b, n, dim)
        return o + o @ W_out

    def _L2_cond_ref(q0, p0, input_drive_seq, coupling, bias):
        import jax, jax.numpy as jnp
        import numpy as np
        DT = 0.01
        EPSILON = 0.08
        ALPHA = 0.7
        BETA = 0.8
        CLAMP = 20.0
        B, T, N = (64, 128, 512)

        def _derivative(q, p, drive, coupling, bias):
            i_couple = jnp.tanh(q) @ coupling.T
            dq = q - q ** 3 / 3.0 - p + drive + i_couple + bias
            dp = EPSILON * (q + ALPHA - BETA * p)
            return (dq, dp)

        def _rk4_step(q, p, drive, coupling, bias):
            dq1, dp1 = _derivative(q, p, drive, coupling, bias)
            dq2, dp2 = _derivative(q + 0.5 * DT * dq1, p + 0.5 * DT * dp1, drive, coupling, bias)
            dq3, dp3 = _derivative(q + 0.5 * DT * dq2, p + 0.5 * DT * dp2, drive, coupling, bias)
            dq4, dp4 = _derivative(q + DT * dq3, p + DT * dp3, drive, coupling, bias)
            q_next = q + DT / 6.0 * (dq1 + 2 * dq2 + 2 * dq3 + dq4)
            p_next = p + DT / 6.0 * (dp1 + 2 * dp2 + 2 * dp3 + dp4)
            q_next = jnp.clip(q_next, -CLAMP, CLAMP)
            p_next = jnp.clip(p_next, -CLAMP, CLAMP)
            return (q_next, p_next)
        drive_tbn = jnp.swapaxes(input_drive_seq, 0, 1)

        def scan_fn(carry, drive):
            q, p = carry
            q, p = _rk4_step(q, p, drive, coupling, bias)
            return ((q, p), q)
        (_, _), q_trace_tbn = jax.lax.scan(scan_fn, (q0, p0), drive_tbn)
        return jnp.swapaxes(q_trace_tbn, 0, 1)

    def _L3_cond_ref(initial_state, inputs, W_ih, W_hh, b_ih, b_hh):
        import jax, jax.numpy as jnp
        import numpy as np
        B, T, D = (16, 128, 512)
        "ScanOverTime(GRU cell): sequential per-timestep module call with\n            dict-state passing; merge_dict_trees stacks the per-step\n            'state_predicted' tensors along axis=1 -> [B, T, D]."

        def cell(h, x):
            gi = x @ W_ih + b_ih
            gh = h @ W_hh + b_hh
            i_r, i_z, i_n = jnp.split(gi, 3, axis=-1)
            h_r, h_z, h_n = jnp.split(gh, 3, axis=-1)
            r = jax.nn.sigmoid(i_r + h_r)
            z = jax.nn.sigmoid(i_z + h_z)
            n = jnp.tanh(i_n + r * h_n)
            h_new = (1.0 - z) * n + z * h
            return (h_new, h_new)
        xs = jnp.swapaxes(inputs, 0, 1)
        _, hs = jax.lax.scan(cell, initial_state, xs)
        return jnp.swapaxes(hs, 0, 1)
    x = x + _L0_cond_ref(fside_BxSx1_0, cond_2048[:, None, :], x, 5120)
    x = x + _L1_cond_ref(x, cond_2048[:, None, :], L1_cond_W_emb, L1_cond_b_emb, L1_cond_g_norm, L1_cond_W_qkv, L1_cond_g_q, L1_cond_g_k, L1_cond_W_out)
    x = x + _L2_cond_ref(cond_2048, cond_2048, x, L2_cond_coupling, L2_cond_bias)
    x = x + _L3_cond_ref(cond_2048, x, L3_cond_W_ih, L3_cond_W_hh, L3_cond_b_ih, L3_cond_b_hh)
    return x

_drawn_inputs = setup_inputs


def setup_inputs(seed=0):
    import zlib

    import numpy as np

    out = dict(_drawn_inputs(seed))
    spreads = {'L1_cond_b_emb': (0.0, 0.1),
     'L1_cond_g_norm': (1.0, 0.2),
     'L1_cond_g_q': (1.0, 0.6),
     'L1_cond_g_k': (1.0, 0.6),
     'L2_cond_bias': (0.0, 0.1),
     'L3_cond_b_ih': (0.0, 0.687),
     'L3_cond_b_hh': (0.0, 0.8)}
    factors = {}
    for name, (base, spread) in spreads.items():
        noise = np.random.default_rng([zlib.crc32(name.encode()), seed]).standard_normal(out[name].shape)
        drawn = base * np.exp(spread * noise) if base else spread * noise
        out[name] = jnp.asarray(drawn.astype(out[name].dtype))
    for name, factor in factors.items():
        out[name] = (out[name] * factor).astype(out[name].dtype)
    return out
```

```python
from contextlib import ExitStack

import concourse.bass as bass
from concourse import mybir

F32 = mybir.dt.float32
F16 = mybir.dt.float16
BF16 = mybir.dt.bfloat16
I32 = mybir.dt.int32
ALU = mybir.AluOpType
ACT = mybir.ActivationFunctionType
AX_X = mybir.AxisListType.X

P = 128
NB, T, D = 4, 512, 512
KC = D // P
TC = T // P
NT = NB * TC
S16 = KC * NB
HEADS, DH = 16, 32
TOPK = 5120
DIAGONAL = -3.0e38
C_QKV, C_OUT, C_IH, C_HH, C_CPL, C_ALL = 0, 1536, 2048, 3584, 5120, 5632
W_PIECE = C_ALL // 4

DT, EPSILON, ALPHA, BETA, CLAMP = 0.01, 0.08, 0.7, 0.8, 20.0
C_STAGE = [0.5 * DT, 0.5 * DT, DT, DT / 6.0]
W_SCALE = 128.0
GB = 8
NG = T // GB
LAG = 2
GH_CUT = [0, 0, 32, 64, 96]
GI_CUT = [0, 0] + [min(96, 14 * k) for k in range(1, GB)]
CPL_EARLY = 16
PRE = 19
PRE_AT = [0, 5, 9, 13]


def mixed_scan_kernel(nc, x, side, condT, cond, W_emb, b_emb, g_norm, g_qk, W_all, bias_l2, b_gates, out):
    ctx = ExitStack()
    with ctx:
        def sb(name, shape, dt=F32):
            return ctx.enter_context(nc.sbuf_tensor(name, shape, dt))

        def sem(name):
            return ctx.enter_context(nc.semaphore(name))

        bank = [ctx.enter_context(nc.psum_tensor(f"bank{i}", [P, 512], F32)) for i in range(8)]

        R_X = sb("R_X", [P, 8192])
        R_A = sb("R_A", [P, 12288])
        R_B = sb("R_B", [P, 4096])
        R_T = sb("R_T", [P, (T + 1) * S16])
        R_H = sb("R_H", [P, 6144])
        W_Q = sb("W_Q", [P, 2, KC, 1536], F16)
        W_O = sb("W_O", [P, 2, KC, 512], F16)

        X = R_X[:, :].rearrange("p (b t d) -> p b t d", b=NB, t=TC)
        ADJ = R_A[:, 0:8192].rearrange("p (b t d) -> p b t d", b=NB, t=TC)
        ADJ_B = R_A[:, 0:8192].rearrange("p (b n) -> p b n", b=NB)
        TRUNC = R_A[:, 8192:12288].bitcast(BF16).rearrange("p (b n) -> p b n", b=NB)
        MASK = R_B[:, 0:2048].bitcast(F16).rearrange("p (u n) -> p u n", u=2)
        TB = R_B[:, 2048:4096].rearrange("p (b d) -> p b d", b=NB)
        STG = R_T[:, 0:2 * W_PIECE].rearrange("p (u n) -> p u n", u=2)
        HALF = R_T[:, 2 * W_PIECE:4 * W_PIECE].bitcast(F16).rearrange("p (u h n) -> p u h n", u=2, h=2)
        WE = R_H[:, 0:4096].rearrange("p (k n) -> p k n", k=KC)
        X1T = R_T[:, 0:T * 16].rearrange("p (t c b) -> p t c b", t=T, c=KC)
        X1F = R_T[:, 0:(T + 1) * 16].rearrange("p (t s) -> p t s", t=T + 1)
        W_HH = R_X[:, 0:6144].bitcast(F16).rearrange("p (h k n) -> p h k n", h=2, k=KC)
        W_CP = R_X[:, 6144:8192].bitcast(F16).rearrange("p (h k n) -> p h k n", h=2, k=KC)
        W_IH = R_A[:, 0:6144].bitcast(F16).rearrange("p (h k n) -> p h k n", h=2, k=KC)

        W16 = nc.dram_tensor("w16_scratch", (P, 2, KC, C_ALL), F16, kind="Internal").ap()
        W16F = W16.rearrange("p h k n -> p h (k n)")
        XN = R_H[:, 0:2048].bitcast(F16).rearrange("p (h k n) -> p h k n", h=2, k=KC)
        OTH = XN
        OT = R_H[:, 2048:4096].rearrange("p (c n) -> p c n", c=KC)
        XB = OT
        QKH = R_H[:, 4096:5120].bitcast(F16).rearrange("p (u h n) -> p u h n", u=2, h=2)
        xnf = R_H[:, 5120:6144].rearrange("p (u n) -> p u n", u=2)
        XH = R_B[:, 0:2048].rearrange("p (t d) -> p t d", t=TC)
        PT = R_B[:, :].rearrange("p (u k n) -> p u k n", u=2, k=KC)
        QS = R_A[:, 0:4096].bitcast(F16).rearrange("p (h n) -> p h n", h=HEADS)
        KS = R_A[:, 4096:8192].bitcast(F16).rearrange("p (h n) -> p h n", h=HEADS)
        V = R_A[:, 8192:12288].rearrange("p (t h e) -> p t h e", t=TC, h=HEADS)
        X1V = R_T[:, 0:T * S16].rearrange("p (t c b) -> p c b t", t=T, c=KC)
        sqf = sb("sqf", [P, 2, 512])
        sd = sb("sd", [P, 2, 512])
        qn = sb("qn", [P, 2, 512])
        ri = sd[:, 0, :]
        identf = sb("identf", [P, P])
        blk32 = sb("blk32", [P, P])
        ident16 = sb("ident16", [P, P], F16)
        ones16 = sb("ones16", [P, 2 * KC * GB * NB], F16)
        M16 = sb("M16", [P, TC, 32], F16)
        sideT = sb("sideT", [P, NT])
        bemb = sb("bemb", [P, 8])
        gn = sb("gn", [P, KC])
        gqk = sb("gqk", [P, 2])
        gqs = sb("gqs", [P, 2])
        mod_a = sb("mod_a", [P, KC, NB])
        mod_b = sb("mod_b", [P, KC, NB])
        nmx = sb("nmx", [P, NT])
        esum = sb("esum", [P, NT])
        rsum = sb("rsum", [P, NT])
        rsc = sb("rsc", [P, NT])
        bitf = sb("bitf", [P, 32])
        biti = sb("biti", [P, 32], I32)
        key = sb("key", [P, NB], I32)
        neg = sb("neg", [P, NB], I32)
        cand = sb("cand", [P, NB], I32)
        addb = sb("addb", [P, NB], I32)
        c16 = sb("c16", [P, NB], F16)
        ssx = sb("ssx", [P, TC])
        stdx = sb("stdx", [P, TC])
        rstd = sb("rstd", [P, TC])
        eps = sb("eps", [P, 1])
        candf = cand[:, :].bitcast(F32)

        sx = [sem(f"x_loaded_{b}") for b in range(NB)]
        s_par = sem("small_loaded")
        s_we = sem("w_emb_loaded")
        s_tb = sem("cond_loaded")
        s_const = sem("constants_ready")
        s_iota = sem("identity_steps")
        s_max = sem("score_max")
        s_exp = sem("score_exp")
        s_rs = sem("score_scales")
        s_adj = sem("scores_ready")
        s_diag = sem("diagonal_out")
        s_trunc = sem("scores_truncated")
        s_mask = sem("mask_ready")
        s_mused = sem("mask_counted")
        s_c16 = sem("counts_copied")
        s_tot = sem("totals_ready")
        s_add = sem("bit_decided")
        s_key = sem("key_ready")
        s_cand = sem("candidate_ready")
        s_bits = sem("bit_table")
        s_wld = [sem(f"piece_loaded_{u}") for u in range(2)]
        s_whi = sem("piece_hi")
        s_wlo = sem("piece_lo")
        s_wst = [sem(f"piece_stored_{u}") for u in range(2)]
        s_wq = sem("projection_weights")
        s_emb = sem("scale_shift_done")
        s_mod = sem("modulation")
        s_modt = sem("modulation_steps")
        s_x0 = sem("x0_ready")
        s_kv = sem("key_value_constants")
        s_xb = sem("x_rows_copied")
        s_ss = sem("row_squares")
        s_std = sem("row_std")
        s_rstd = sem("row_rstd")
        s_xhat = sem("x_hat")
        s_raw = sem("x_transposed")
        s_rawE = sem("x_transposed_out")
        s_xT = sem("x_hat_transposed")
        s_xnf = sem("x_normed")
        s_xnh = sem("x_normed_hi")
        s_xn = sem("x_normed_halves")
        s_qk = sem("qk_projected")
        s_sqf = sem("qk_squared")
        s_ssq = sem("qk_squares_summed")
        s_sd = sem("qk_std")
        s_rr = sem("qk_rstd")
        s_qn = sem("qk_normed")
        s_qh = sem("qk_hi")
        s_ql = sem("qk_lo")
        s_qks = [sem(f"qk_stacked_{c}") for c in range(8)]
        s_v = sem("v_projected")
        s_ve = sem("v_ready")
        s_a = sem("logits_rows")
        s_mx = sem("row_max")
        s_mt = sem("max_transposed")
        s_mc = sem("max_stacked")
        s_st = sem("logits_columns")
        s_e = sem("attention_weights")
        s_av = sem("values_summed")
        s_ri = sem("softmax_sums")
        s_ao = sem("attention_out")
        s_oh = sem("attention_hi")
        s_ol = sem("attention_lo")
        s_y = sem("out_projected")
        s_ye = sem("out_projection_read")
        s_x1 = sem("x1_ready")

        cT = sb("cT", [P, S16])
        bl2 = sb("bl2", [P, S16])
        bg24 = sb("bg24", [P, 24])
        BIASB = sb("BIASB", [P, 12, GB * NB])
        ones = sb("ones", [P, GB * NB])

        TT = sb("TT", [P, KC, 2, NB], F16)
        HH = sb("HH", [P, KC, 2, NB], F16)
        tf = sb("tf", [P, S16])
        sq = sb("sq", [P, S16])
        zc = sb("zc", [P, 32])
        dd = sb("dd", [P, 2, 32])
        dt6 = sb("dt6", [P, 32])
        x2f = sb("x2f", [P, S16])
        dd6 = sb("dd6", [P, 2, 32])
        wa = sb("wa", [P, 32])
        wb = sb("wb", [P, 32])
        w4 = sb("w4", [P, 32])
        e1 = sb("e1", [P, 32])
        e2 = sb("e2", [P, 32])
        e3 = sb("e3", [P, 32])
        gq = sb("gq", [P, S16])
        gp = sb("gp", [P, S16])
        ncub = sb("ncub", [P, S16])
        base = sb("base", [P, S16])
        part = sb("part", [P, S16])
        XGn = sb("XGn", [P, KC, 2, GB, NB], F16)
        XGc = sb("XGc", [P, KC, 2, GB, NB], F16)
        gie = sb("gie", [P, 4, GB * NB])
        GIn = sd[:, 1, 0:384].rearrange("p (n c) -> p n c", n=12)
        GIc = sd[:, 0, :].rearrange("p (n c) -> p n c", n=16)
        nr1 = sb("nr1", [P, 32])
        nr = sb("nr", [P, 32])
        zg1 = sb("zg1", [P, S16])
        zg = sb("zg", [P, S16])
        rg = sb("rg", [P, S16])
        zs = sb("zs", [P, S16])
        rn = sb("rn", [P, S16])
        npre = sb("npre", [P, S16])
        ng = sb("ng", [P, S16])
        hd = sb("hd", [P, S16])
        zd = sb("zd", [P, S16])
        hst = sb("hst", [P, S16])

        Z = sb("Z", [P, 128])
        QP = bank[0][:, 0:S16]
        zz = [Z[:, 32 * s:32 * s + 32] for s in range(4)]
        qq = [Z[:, 32 * s:32 * s + 16] for s in range(4)]
        pp = [Z[:, 32 * s + 16:32 * s + 32] for s in range(4)]
        CPL = bank[1][:, 0:32].rearrange("p (h j b) -> p h j b", h=2, j=KC)
        GHN = bank[2][:, 0:64].rearrange("p (h n b) -> p h n b", h=2, n=8)
        GHZ = bank[5][:, 0:32].rearrange("p (h n b) -> p h n b", h=2, n=4)
        GI = [bank[i][:, 0:256].rearrange("p (n h c) -> p n h c", n=4, h=2) for i in (3, 4, 6)]


        def v4(a):
            return a.rearrange("p (c b) -> p c b", b=NB)

        s_prep = sem("scan_params_ready")
        s_wl = sem("scan_weights_loaded")
        s_q = sem("q_ready")
        s_qs = sem("q_stored")
        s_t1 = sem("tanh_hi_ready")
        s_tf = sem("tanh_ready")
        s_sq = sem("square_ready")
        s_t2 = sem("tanh_lo_ready")
        s_cp = sem("couple_ready")
        s_pre = sem("vec_pre")
        s_clip = sem("state_clipped")
        s_dd = sem("drive_ready")
        s_dsum = sem("drive_summed")
        s_x2 = sem("x2_ready")
        s_xf = sem("x2_full_ready")
        s_xh = sem("x2_hi_ready")
        s_xl = sem("x2_lo_ready")
        s_xg = sem("x2_group_ready")
        s_gim = sem("gi_matmuls_done")
        s_gie = sem("gi_half_summed")
        s_gin = sem("gi_next_ready")
        s_gic = sem("gi_current_ready")
        s_ghnr = sem("gh_nr_done")
        s_ghz = sem("gh_z_done")
        s_ones = sem("ones_ready")
        s_nr1 = sem("nr_half")
        s_nr = sem("nr_ready")
        s_r = sem("r_ready")
        s_rn = sem("rn_ready")
        s_np = sem("n_pre_ready")
        s_n = sem("n_ready")
        s_zg1 = sem("z_half")
        s_zg = sem("z_pre_ready")
        s_z = sem("z_ready")
        s_hd = sem("h_minus_n")
        s_zd = sem("z_h_minus_n")
        s_h = sem("h_ready")
        s_h1 = sem("h_hi_ready")
        s_h2 = sem("h_lo_ready")
        s_o = sem("out_ready")
        s_out = sem("out_written")

        GH_MM = [(half, k, wblk + j, slot + j)
                 for slot, wblk in ((0, 8), (4, 0), (8, 4)) for half in (1, 0) for j in range(4) for k in range(KC)]
        GI_MM = [(half, k, wblk + j) for wblk in (0, 4, 8) for j in range(4) for half in (1, 0) for k in range(KC)]

        def groups(eng, body):
            for g in range(3):
                body(g, True, g >= 1, g >= LAG, g > LAG)
            with eng.Fori(3, NG) as g:
                body(g, True, True, True, True)
            body(NG, False, True, True, True)
            body(NG + 1, False, False, True, True)

        SPLIT_MM = [(hw, hx, c) for hw, hx in ((0, 0), (0, 1), (1, 0)) for c in range(KC)]
        ST_BANK = [2, 3, 4]
        PIECES = 4 * KC

        block = ctx.enter_context(nc.Block())

        @block.tensor
        def _(pe):
            def scan_group(g, rk, gi, gru, tail):
                for k in range(GB):
                    n = g * GB + k
                    m = n - LAG * GB
                    for s in range(4):
                        if rk:
                            pe.wait_ge(s_t1, n * 4 + (s + 1))
                            if not (isinstance(n, int) and n == 0 and s == 0):
                                pe.wait_ge(s_qs, n * 4 + s)
                            low = [(j, c) for j in range(KC) for c in range(KC)]
                            for i, (j, c) in enumerate(low[:CPL_EARLY]):
                                pe.matmul(CPL[:, 0, j, :], W_CP[:, 1, c, j * P:(j + 1) * P], TT[:, c, 0, :],
                                          start=(i == 0), stop=False, skip_group_check=True)
                            pe.wait_ge(s_t2, n * 4 + (s + 1))
                            for j in range(KC):
                                for c in range(KC):
                                    mm = pe.matmul(CPL[:, :, j, :], W_CP[:, 0, c, j * P:(j + 1) * P], TT[:, c, :, :],
                                                   start=False, stop=False, skip_group_check=True)
                            for i, (j, c) in enumerate(low[CPL_EARLY:]):
                                mm = pe.matmul(CPL[:, 0, j, :], W_CP[:, 1, c, j * P:(j + 1) * P], TT[:, c, 0, :],
                                               start=False, stop=(i == len(low) - CPL_EARLY - 1), skip_group_check=True)
                            mm.then_inc(s_cp, 1)
                        if gi and s == 0 and k:
                            if k == 1:
                                pe.wait_ge(s_xg, g)
                                if tail or gru:
                                    pe.wait_ge(s_gin, g * 3 - 3)
                            for i in range(GI_CUT[k], GI_CUT[k + 1] if k < GB - 1 else 96):
                                half, c, blk = GI_MM[i]
                                o = GI[blk // 4][:, blk % 4]
                                if half:
                                    mm = pe.matmul(o[:, 0, :], W_IH[:, 1, c, blk * P:(blk + 1) * P], XGc[:, c, 0],
                                                   start=(blk % 4 == 0 and c == 0), stop=False, skip_group_check=True)
                                else:
                                    mm = pe.matmul(o, W_IH[:, 0, c, blk * P:(blk + 1) * P], XGc[:, c],
                                                   start=False, stop=(c == KC - 1), skip_group_check=True)
                                if i % 32 == 31:
                                    mm.then_inc(s_gim, 1)
                        if gru:
                            for i in range(GH_CUT[s], GH_CUT[s + 1]):
                                half, c, wblk, slot = GH_MM[i]
                                if i == 0:
                                    pe.wait_ge(s_h1, m + 1)
                                if i == 16:
                                    pe.wait_ge(s_h2, m + 1)
                                o = GHN[:, :, slot] if slot < 8 else GHZ[:, :, slot - 8]
                                if half:
                                    mm = pe.matmul(o[:, 0], W_HH[:, 1, c, wblk * P:(wblk + 1) * P], HH[:, c, 0],
                                                   start=(i in (0, 64)), stop=False, skip_group_check=True)
                                else:
                                    mm = pe.matmul(o, W_HH[:, 0, c, wblk * P:(wblk + 1) * P], HH[:, c],
                                                   start=False, stop=(c == KC - 1), skip_group_check=True)
                                if i == 63:
                                    mm.then_inc(s_ghnr, 1)
                                if i == 95:
                                    mm.then_inc(s_ghz, 1)

            pe.wait_ge(s_par, 16 * 7)
            pe.wait_ge(s_we, 16)
            for n in range(8):
                for c in range(KC):
                    mm = pe.matmul(bank[4][:, n * NB:(n + 1) * NB], WE[:, c, n * P:(n + 1) * P],
                                   cT[:, c * NB:(c + 1) * NB], start=(c == 0), stop=(c == KC - 1))
            mm.then_inc(s_emb, 1)

            def count(e, pair, after_unread=False):
                for j in range(2):
                    pe.wait_ge(s_mask, e * 2 + (j + 1))
                    if j == 0 and after_unread:
                        pe.wait_ge(s_c16, e)
                    for t in range(16):
                        mm = pe.matmul(bank[pair][:, j:j + 1], MASK[:, j, t * P:(t + 1) * P], ones16[:, 0:1],
                                       start=(t == 0), stop=(t == 15))
                    mm.then_inc(s_mused, 1)
                pe.wait_ge(s_mused, e * 2 + 2)
                pe.wait_ge(s_c16, e + 1)
                pe.matmul(bank[2 + pair][:, 0:2], ones16[:, 0:P], c16[:, 2 * pair:2 * pair + 2],
                          start=True, stop=True).then_inc(s_tot, 1)

            pe.wait_ge(s_const, 1)
            count(0, 0)
            count(1, 1)
            count(2, 0)
            count(3, 1)
            count(4, 0)
            with pe.Fori(0, 14) as i:
                count(i * 2 + 5, 1)
                count(i * 2 + 6, 0)
            count(33, 0, True)
            with pe.Fori(0, 16) as i:
                count(i * 2 + 34, 1)
                count(i * 2 + 35, 0)

            pe.wait_ge(s_wq, 32)
            pe.wait_ge(s_kv, 2)
            with pe.Fori(0, NB) as b:
                pe.wait_ge(s_xb, b * 4 + 4)
                pe.wait_ge(s_ye, b * 4 + 4)
                for c in range(KC):
                    if c >= 2:
                        pe.wait_ge(s_rawE, b * 4 + (c - 1))
                    for t in range(TC):
                        mm = pe.transpose(bank[c % 2][:, t * P:(t + 1) * P], XB[:, t, c * P:(c + 1) * P], identf[:, :])
                    mm.then_inc(s_raw, 1)
                pe.wait_ge(s_xhat, b * 4 + 4)
                for c in range(KC):
                    if c >= 2:
                        pe.wait_ge(s_xnf, b * 4 + (c - 1))
                    for t in range(TC):
                        mm = pe.transpose(bank[2 + c % 2][:, t * P:(t + 1) * P], XH[:, t, c * P:(c + 1) * P], identf[:, :])
                    mm.then_inc(s_xT, 1)

                def square_sum(cc):
                    pe.wait_ge(s_sqf, b * 8 + (cc + 1))
                    if cc >= 2:
                        pe.wait_ge(s_sd, b * 8 + (cc - 1))
                    pe.matmul(bank[6 + cc % 2][:, :], blk32[:, :], sqf[:, cc % 2, :],
                              start=True, stop=True).then_inc(s_ssq, 1)

                pe.wait_ge(s_xn, b * 4 + 4)
                for cc in range(8):
                    if cc >= 2:
                        pe.wait_ge(s_qn, b * 8 + (cc - 1))
                    col = 512 * (cc % 2) + P * (cc // 2)
                    for i, (hw, hx, c) in enumerate(SPLIT_MM):
                        mm = pe.matmul(bank[4 + cc % 2][:, :], W_Q[:, hw, c, col:col + P], XN[:, hx, c, :],
                                       start=(i == 0), stop=(i == 11))
                    mm.then_inc(s_qk, 1)
                    if cc:
                        square_sum(cc - 1)
                square_sum(7)
                for t in range(TC):
                    if t < 2:
                        pe.wait_ge(s_qn, b * 8 + (7 + t))
                    else:
                        pe.wait_ge(s_ve, b * 4 + (t - 1))
                    for i, (hw, hx, c) in enumerate(SPLIT_MM):
                        mm = pe.matmul(bank[4 + t % 2][:, :], XN[:, hx, c, t * P:(t + 1) * P], W_Q[:, hw, c, 1024:1536],
                                       start=(i == 0), stop=(i == 11))
                    mm.then_inc(s_v, 1)

                def logits_rows(h):
                    if h % 4 == 0:
                        pe.wait_ge(s_qks[h // 2], b * 192 + 192)
                        pe.wait_ge(s_qks[h // 2 + 1], b * 192 + 192)
                    for t in range(TC):
                        if h == 0 and t < 2:
                            pe.wait_ge(s_rawE, b * 4 + 4)
                        else:
                            pe.wait_ge(s_mx, b * 64 + (4 * h + t - 1))
                        pe.matmul(bank[t % 2][:, :], QS[0:96, h, t * P:(t + 1) * P], KS[0:96, h, :],
                                  start=True, stop=True).then_inc(s_a, 1)

                def max_to_row(h):
                    pe.wait_ge(s_mx, b * 64 + (4 * h + 4))
                    if h == 0:
                        pe.wait_ge(s_ve, b * 4 + 4)
                    else:
                        pe.wait_ge(s_mc, b * 16 + h)
                    for t in range(TC):
                        mm = pe.transpose(bank[5][96:128, :].bitcast(F16)[:, t * P:(t + 1) * P], M16[:, t, :], ident16[:, :])
                    mm.then_inc(s_mt, 1)

                def logits_columns(h, t):
                    n = 4 * h + t
                    if t == 0:
                        pe.wait_ge(s_mc, b * 16 + (h + 1))
                    if n < 3:
                        pe.wait_ge(s_xnf, b * 4 + 4)
                    else:
                        pe.wait_ge(s_e, b * 64 + (n - 2))
                    pe.matmul(bank[ST_BANK[n % 3]][:, :], KS[:, h, t * P:(t + 1) * P], QS[:, h, :],
                              start=True, stop=True).then_inc(s_st, 1)

                def sum_values(h, t):
                    if t == 0:
                        if h < 2:
                            pe.wait_ge(s_sd, b * 8 + 8)
                        else:
                            pe.wait_ge(s_ao, b * 16 + (h - 1))
                    pe.wait_ge(s_e, b * 64 + (4 * h + t + 1))
                    mm = pe.matmul(bank[6 + h % 2][0:64, :], V[:, t, h, :], PT[:, h % 2, t, :],
                                   start=(t == 0), stop=(t == 3))
                    if t == 3:
                        mm.then_inc(s_av, 1)

                logits_rows(0)
                for h in range(HEADS + 1):
                    if h:
                        sum_values(h - 1, 0)
                    if h < HEADS:
                        max_to_row(h)
                    if h:
                        sum_values(h - 1, 1)
                    if h < HEADS:
                        logits_columns(h, 0)
                        logits_columns(h, 1)
                    if h:
                        sum_values(h - 1, 2)
                    if h < HEADS:
                        logits_columns(h, 2)
                    if h:
                        sum_values(h - 1, 3)
                    if h < HEADS:
                        logits_columns(h, 3)
                    if h + 1 < HEADS:
                        logits_rows(h + 1)

                pe.wait_ge(s_ol, b * 4 + 4)
                for n in range(KC):
                    if n < 2:
                        pe.wait_ge(s_mx, b * 64 + 64)
                    else:
                        pe.wait_ge(s_ye, b * 4 + (4 + n - 1))
                    for i, (hw, hx, c) in enumerate(SPLIT_MM):
                        mm = pe.matmul(bank[n % 2][:, :], W_O[:, hw, c, n * P:(n + 1) * P], OTH[:, hx, c, :],
                                       start=(i == 0), stop=(i == 11))
                    mm.then_inc(s_y, 1)

            pe.wait_ge(s_wl, 48)
            groups(pe, scan_group)

        @block.scalar
        def _(act):
            def truncate(i):
                b, t = i // TC, i % TC
                act.wait_ge(s_diag, i + 1)
                act.activation(TRUNC[:, b, t * D:(t + 1) * D],
                               ADJ[:, b, t, :].bitcast(BF16).rearrange("p (n e) -> p e n", e=2)[:, 1, :],
                               ACT.Copy).then_inc(s_trunc, 1)

            def scan_group(g, rk, gi, gru, tail):
                for k in range(GB):
                    n = g * GB + k
                    m = n - LAG * GB
                    after = tail or (gru and k > 0)
                    for s in range(4):
                        if rk:
                            act.wait_ge(s_q, n * 4 + (s + 1))
                            act.activation(TT[:, :, 0, :], v4(QP), ACT.Tanh).then_inc(s_t1, 1)
                            act.activation(tf[:, :], QP, ACT.Tanh).then_inc(s_tf, 1)
                            if s == 0:
                                act.wait_ge(s_clip, n + 1)
                            act.activation(sq[:, :], zc[:, 0:16] if s == 0 else QP, ACT.Square,
                                           scale=(C_STAGE[s] / 3.0) ** 0.5).then_inc(s_sq, 1)
                        if gru and k == 0 and s == 1:
                            act.wait_ge(s_gin, g * 3 - 3)
                            if tail:
                                act.wait_ge(s_zg, m)
                            act.activation(GIc[:, 4:16, :], GIn[:, :, :], ACT.Copy).then_inc(s_gic, 1)
                        if after and s == 0:
                            act.wait_ge(s_np, m)
                            act.activation(ng[:, :], npre[:, :], ACT.Tanh).then_inc(s_n, 1)
                            act.wait_ge(s_zg, m)
                            act.activation(zs[:, :], zg[:, :], ACT.Sigmoid).then_inc(s_z, 1)
                        if after and s == 1:
                            act.wait_ge(s_h, m + 1)
                            act.activation(HH[:, :, 0, :], v4(hst[:, :]), ACT.Copy).then_inc(s_h1, 1)
                        if gru and s == 3:
                            act.wait_ge(s_nr, m + 1)
                            act.activation(rg[:, :], nr[:, 16:32], ACT.Sigmoid).then_inc(s_r, 1)

            for i in range(NT):
                b, t = i // TC, i % TC
                act.wait_ge(s_max, i + 1)
                act.activation(ADJ[:, b, t, :], X[:, b, t, :], ACT.Exp, bias=nmx[:, i:i + 1],
                               accum_out=esum[:, i:i + 1]).then_inc(s_exp, 1)
                if i >= 6:
                    truncate(i - 6)
            for i in range(NT - 6, NT):
                truncate(i)

            def copy_counts(e, pair):
                act.wait_ge(s_mused, e * 2 + 2)
                act.activation(c16[:, 2 * pair:2 * pair + 2], bank[pair][:, 0:2], ACT.Copy).then_inc(s_c16, 1)

            def weight_hi(i, u, first=False):
                act.wait_ge(s_wld[u], i * 16 + 16)
                if not first:
                    act.wait_ge(s_wst[u], i * 16)
                act.activation(HALF[:, u, 0, :], STG[:, u, :], ACT.Copy, scale=W_SCALE).then_inc(s_whi, 1)

            for e in range(2):
                copy_counts(e, e % 2)
            for u in range(2):
                weight_hi(0, u, True)
            for e in range(2, 5):
                copy_counts(e, e % 2)
            with act.Fori(0, 7) as i:
                copy_counts(i * 4 + 5, 1)
                copy_counts(i * 4 + 6, 0)
                weight_hi(i + 1, 0)
                copy_counts(i * 4 + 7, 1)
                copy_counts(i * 4 + 8, 0)
                weight_hi(i + 1, 1)
            copy_counts(33, 0)
            with act.Fori(0, 16) as i:
                copy_counts(i * 2 + 34, 1)
                copy_counts(i * 2 + 35, 0)

            act.wait_ge(s_x0, NT)
            act.wait_ge(s_ye, 4)
            with act.Fori(0, NB) as b:
                for t in range(TC):
                    act.activation((sqf, sd)[t // 2][:, t % 2, :], X[:, b, t, :], ACT.Square,
                                   accum_out=ssx[:, t:t + 1]).then_inc(s_ss, 1)
                act.wait_ge(s_ss, b * 4 + 4)
                act.activation(stdx[:, :], ssx[:, :], ACT.Sqrt, bias=eps[:, 0:1], scale=1.0 / D).then_inc(s_std, 1)
                act.wait_ge(s_rstd, b + 1)
                for c in range(KC):
                    act.wait_ge(s_raw, b * 4 + (c + 1))
                    act.activation(X1V[:, c, b, :], bank[c % 2][:, :], ACT.Copy).then_inc(s_rawE, 1)
                    if c == 0:
                        for t in range(TC):
                            act.activation(XH[:, t, :], X[:, b, t, :], ACT.Copy, scale=rstd[:, t:t + 1]).then_inc(s_xhat, 1)
                for c in range(KC):
                    act.wait_ge(s_xnf, b * 4 + (c + 1))
                    act.activation(XN[:, 0, c, :], xnf[:, c % 2, :], ACT.Copy).then_inc(s_xnh, 1)
                for cc in range(10):
                    if cc < 8:
                        act.wait_ge(s_qk, b * 8 + (cc + 1))
                        if cc >= 2:
                            act.wait_ge(s_ssq, b * 8 + (cc - 1))
                        act.activation(sqf[:, cc % 2, :], bank[4 + cc % 2][:, :], ACT.Square,
                                       scale=1.0 / W_SCALE).then_inc(s_sqf, 1)
                    if 1 <= cc <= 8:
                        act.wait_ge(s_ssq, b * 8 + cc)
                        if cc >= 3:
                            act.wait_ge(s_qn, b * 8 + (cc - 2))
                        act.activation(sd[:, (cc - 1) % 2, :], bank[6 + (cc - 1) % 2][:, :], ACT.Sqrt,
                                       bias=eps[:, 0:1], scale=1.0 / DH).then_inc(s_sd, 1)
                    if cc >= 2:
                        act.wait_ge(s_qn, b * 8 + (cc - 1))
                        if cc >= 4:
                            act.wait_ge(s_qks[cc - 4], b * 192 + 192)
                        act.activation(QKH[:, cc % 2, 0, :], qn[:, cc % 2, :], ACT.Copy).then_inc(s_qh, 1)
                for t in range(TC):
                    act.wait_ge(s_v, b * 4 + (t + 1))
                    act.activation(V[:, t, :, 0:DH], bank[4 + t % 2][:, :].rearrange("p (h d) -> p h d", h=HEADS),
                                   ACT.Copy, scale=1.0 / W_SCALE).then_inc(s_ve, 1)

                def attention_hi(c):
                    act.wait_ge(s_ao, b * 16 + (4 * c + 4))
                    act.activation(OTH[:, 0, c, :], OT[:, c, :], ACT.Copy).then_inc(s_oh, 1)

                for h in range(HEADS):
                    act.wait_ge(s_mt, b * 16 + (h + 1))
                    act.activation(QS[96:128, h, :], bank[5][96:128, :].bitcast(F16)[:, 0:512], ACT.Copy).then_inc(s_mc, 1)
                    for t in range(TC):
                        act.wait_ge(s_st, b * 64 + (4 * h + t + 1))
                        if t == 0 and h >= 2:
                            act.wait_ge(s_av, b * 16 + (h - 1))
                        act.activation(PT[:, h % 2, t, :], bank[ST_BANK[(4 * h + t) % 3]][:, :], ACT.Exp,
                                       scale=float(DH) ** -0.5).then_inc(s_e, 1)
                    if h % 4 == 1 and h > 1:
                        attention_hi(h // 4 - 1)
                attention_hi(3)

            act.wait_ge(s_prep, 1)
            act.activation(HH[:, :, 0, :], v4(cT[:, :]), ACT.Copy).then_inc(s_h1, 1)
            groups(act, scan_group)
            act.wait_ge(s_np, T)
            act.activation(ng[:, :], npre[:, :], ACT.Tanh).then_inc(s_n, 1)
            act.wait_ge(s_zg, T)
            act.activation(zs[:, :], zg[:, :], ACT.Sigmoid).then_inc(s_z, 1)

        @block.vector
        def _(v):
            def evacuate_gi(g, gate, first):
                src = GI[gate]
                v.wait_ge(s_gim, g * 3 - 2 + gate)
                if gate == 0 and not first:
                    v.wait_ge(s_gic, g - 1)
                v.scalar_tensor_tensor(out=gie[:, :, :], in0=src[:, :, 1, :], scalar=1.0 / W_SCALE,
                                       in1=BIASB[:, 4 * gate:4 * gate + 4, :], op0=ALU.mult, op1=ALU.add).then_inc(s_gie, 1)
                v.wait_ge(s_gie, g * 3 - 2 + gate)
                v.scalar_tensor_tensor(out=GIn[:, 4 * gate:4 * gate + 4, :], in0=src[:, :, 0, :], scalar=1.0 / W_SCALE,
                                       in1=gie[:, :, :], op0=ALU.mult, op1=ALU.add).then_inc(s_gin, 1)

            def tanh_low(count):
                v.wait_ge(s_t1, count)
                v.wait_ge(s_tf, count)
                v.tensor_tensor(TT[:, :, 1, :], v4(tf[:, :]), TT[:, :, 0, :], ALU.subtract).then_inc(s_t2, 1)

            def gru_n(m, t):
                v.wait_ge(s_rn, m + 1)
                v.tensor_tensor(v4(npre[:, :]), v4(rn[:, :]), GIc[:, 12:16, t * NB:(t + 1) * NB],
                                ALU.add).then_inc(s_np, 1)

            def scores(b):
                four = slice(b * TC, (b + 1) * TC)
                v.wait_ge(s_exp, (b + 1) * TC)
                v.reciprocal(rsum[:, four], esum[:, four]).then_inc(s_rs, 1)
                if b == 0:
                    v.wait_ge(s_par, 16 * 7)
                    v.wait_ge(s_tb, 16)
                v.wait_ge(s_rs, 2 * b + 1)
                v.scalar_tensor_tensor(out=rsc[:, four], in0=rsum[:, four], scalar=float(D) ** -0.5,
                                       in1=sideT[:, four], op0=ALU.mult, op1=ALU.mult).then_inc(s_rs, 1)
                v.wait_ge(s_rs, 2 * b + 2)
                for t in range(TC):
                    i = b * TC + t
                    v.scalar_tensor_tensor(out=ADJ[:, b, t, :], in0=ADJ[:, b, t, :], scalar=rsc[:, i:i + 1],
                                           in1=TB[:, b, :], op0=ALU.mult, op1=ALU.mult).then_inc(s_adj, 1)

            def cubic(count, c, q_s):
                v.wait_ge(s_sq, count)
                return v.scalar_tensor_tensor(out=ncub[:, :], in0=sq[:, :], scalar=c, in1=q_s,
                                              op0=ALU.subtract, op1=ALU.mult)

            def gru_z_half(m, t):
                v.wait_ge(s_ghz, m + 1)
                v.scalar_tensor_tensor(out=v4(zg1[:, :]), in0=GHZ[:, 1], scalar=1.0 / W_SCALE,
                                       in1=GIc[:, 8:12, t * NB:(t + 1) * NB], op0=ALU.mult, op1=ALU.add).then_inc(s_zg1, 1)

            def gru_z(m):
                v.wait_ge(s_zg1, m + 1)
                v.scalar_tensor_tensor(out=v4(zg[:, :]), in0=GHZ[:, 0], scalar=1.0 / W_SCALE,
                                       in1=v4(zg1[:, :]), op0=ALU.mult, op1=ALU.add).then_inc(s_zg, 1)

            def scan_group(g, rk, gi, gru, tail):
                for k in range(GB):
                    n = g * GB + k
                    m = n - LAG * GB
                    after = tail or (gru and k > 0)
                    static = isinstance(n, int)
                    pre = [n * PRE]

                    def done(ins):
                        ins.then_inc(s_pre, 1)
                        pre[0] = pre[0] + 1
                        return pre[0]

                    for s in range(4):
                        c = C_STAGE[s]
                        w = [wa, wa, wb, w4][s]
                        q_s = zc[:, 0:16] if s == 0 else qq[s]
                        p_s = zc[:, 16:32] if s == 0 else pp[s]
                        if (rk or (k == 0 and gi)) and s == 0:
                            if static and n == 0:
                                v.tensor_copy(zc[:, :], zz[0]).then_inc(s_clip, 1)
                            else:
                                v.wait_ge(s_qs, n * 4)
                                if not (static and n < 2):
                                    v.wait_ge(s_x2, n - 1)
                                v.tensor_scalar(zc[:, :], zz[0], -CLAMP, CLAMP, ALU.max, ALU.min).then_inc(s_clip, 1)
                        if rk and s == 0:
                            tanh_low(n * 4 + 1)
                            v.wait_ge(s_clip, n + 1)
                            v.wait_ge(s_dd, n + 1)
                            v.scalar_tensor_tensor(out=wa[:, :], in0=dd[:, k % 2, :], scalar=0.5 * DT, in1=zc[:, :],
                                                   op0=ALU.mult, op1=ALU.add)
                            w_done = done(v.scalar_tensor_tensor(out=wb[:, :], in0=dd[:, k % 2, :], scalar=DT,
                                                                 in1=zc[:, :], op0=ALU.mult, op1=ALU.add))
                        if rk and s:
                            v.wait_ge(s_qs, n * 4 + s)
                        if rk and s == 1:
                            v.tensor_tensor(e1[:, :], zz[1], zc[:, :], ALU.subtract)
                        if rk and s == 2:
                            v.scalar_tensor_tensor(out=e2[:, :], in0=zz[2], scalar=2.0, in1=e1[:, :],
                                                   op0=ALU.mult, op1=ALU.add)
                        if rk and s == 3:
                            e_done = done(v.tensor_tensor(e3[:, :], zz[3], e2[:, :], ALU.add))
                            tanh_low(n * 4 + 4)
                            v.wait_ge(s_pre, e_done)
                            w_done = done(v.scalar_tensor_tensor(out=w4[:, :], in0=e3[:, :], scalar=1.0 / 3.0,
                                                                 in1=dd6[:, k % 2, :], op0=ALU.mult, op1=ALU.add))
                        if gru and s == 3:
                            v.wait_ge(s_ghnr, m + 1)
                            if k == 0:
                                v.wait_ge(s_gic, g - 1)
                            v.scalar_tensor_tensor(out=nr1[:, :].rearrange("p (n b) -> p n b", b=NB), in0=GHN[:, 1],
                                                   scalar=1.0 / W_SCALE, in1=GIc[:, 0:8, k * NB:(k + 1) * NB],
                                                   op0=ALU.mult, op1=ALU.add).then_inc(s_nr1, 1)
                        if after and s == 0:
                            gru_z_half(m - 1, (k - 1) % GB)
                            gru_n(m - 1, (k - 1) % GB)
                        if rk and s in (0, 3):
                            n_done = done(cubic(n * 4 + (s + 1), c, q_s))
                            v.wait_ge(s_pre, w_done)
                        if rk:
                            v.scalar_tensor_tensor(out=gq[:, :], in0=p_s, scalar=-c, in1=w[:, 0:16],
                                                   op0=ALU.mult, op1=ALU.add)
                            h_done = done(v.scalar_tensor_tensor(out=gp[:, :], in0=p_s, scalar=-c * EPSILON * BETA,
                                                                 in1=w[:, 16:32], op0=ALU.mult, op1=ALU.add))
                        if rk and s in (1, 2):
                            tanh_low(n * 4 + (s + 1))
                        if gru and s == 3:
                            v.wait_ge(s_nr1, m + 1)
                            v.scalar_tensor_tensor(out=nr[:, :].rearrange("p (n b) -> p n b", b=NB), in0=GHN[:, 0],
                                                   scalar=1.0 / W_SCALE, in1=nr1[:, :].rearrange("p (n b) -> p n b", b=NB),
                                                   op0=ALU.mult, op1=ALU.add).then_inc(s_nr, 1)
                        if after and s == 0:
                            gru_z(m - 1)
                        if rk:
                            v.wait_ge(s_pre, h_done)
                            v.scalar_tensor_tensor(out=pp[(s + 1) % 4], in0=q_s, scalar=c * EPSILON, in1=gp[:, :],
                                                   op0=ALU.mult, op1=ALU.add)
                        if rk and s in (1, 2):
                            n_done = done(cubic(n * 4 + (s + 1), c, q_s))
                        if rk:
                            v.wait_ge(s_pre, n_done)
                            b_done = done(v.tensor_tensor(base[:, :], gq[:, :], ncub[:, :], ALU.subtract))
                        if gi and (k, s) in ((4, 1), (6, 1), (7, 2)):
                            evacuate_gi(g, {4: 0, 6: 1, 7: 2}[k], not gru)
                        if rk:
                            v.wait_ge(s_cp, n * 4 + (s + 1))
                            v.wait_ge(s_pre, b_done)
                            u_done = done(v.scalar_tensor_tensor(out=v4(part[:, :]), in0=CPL[:, 1], scalar=c / W_SCALE,
                                                                 in1=v4(base[:, :]), op0=ALU.mult, op1=ALU.add))
                            v.wait_ge(s_pre, u_done)
                            v.scalar_tensor_tensor(out=v4(QP), in0=CPL[:, 0], scalar=c / W_SCALE,
                                                   in1=v4(part[:, :]), op0=ALU.mult, op1=ALU.add).then_inc(s_q, 1)
                            v.scalar_tensor_tensor(out=v4(qq[(s + 1) % 4]), in0=CPL[:, 0], scalar=c / W_SCALE,
                                                   in1=v4(part[:, :]), op0=ALU.mult, op1=ALU.add).then_inc(s_qs, 1)
                        if gru and s == 3:
                            v.wait_ge(s_r, m + 1)
                            v.tensor_tensor(rn[:, :], rg[:, :], nr[:, 0:16], ALU.mult).then_inc(s_rn, 1)

            for b in range(NB):
                v.wait_ge(sx[b], 16)
                for t in range(TC):
                    i = b * TC + t
                    v.reduce_max(nmx[:, i:i + 1], X[:, b, t, :], AX_X, negate=True).then_inc(s_max, 1)
                if b:
                    scores(b - 1)
            scores(NB - 1)
            v.wait_ge(s_emb, 1)
            for c in range(KC):
                v.tensor_scalar(mod_b[:, c, :], bank[4][:, (4 + c) * NB:(5 + c) * NB], bemb[:, 4 + c:5 + c], None, ALU.add)
                v.tensor_scalar(mod_a[:, c, :], bank[4][:, c * NB:(c + 1) * NB], bemb[:, c:c + 1], 1.0,
                                ALU.add, ALU.add).then_inc(s_modt, 1)
            v.wait_ge(s_modt, KC)
            for c in range(KC):
                v.tensor_scalar(mod_a[:, c, :], mod_a[:, c, :], gn[:, c:c + 1], None, ALU.mult)
            v.tensor_scalar(gqs[:, :], gqk[:, :], 1.0 / W_SCALE, None, ALU.mult)

            v.wait_ge(s_bits, 1)
            v.tensor_copy(biti[:, :], bitf[:, :])
            v.memset(key[:, :], 0)
            v.memset(cand[:, :], 0).then_inc(s_cand, 1)

            def compare(e, pair):
                for j in range(2):
                    v.wait_ge(s_cand, 1)
                    if e:
                        v.wait_ge(s_mused, e * 2 + (j - 1))
                    b = 2 * pair + j
                    v.tensor_scalar(MASK[:, j, :], ADJ_B[:, b, :], candf[:, b:b + 1], None, ALU.is_ge).then_inc(s_mask, 1)

            v.wait_ge(s_diag, NT)
            compare(0, 0)
            compare(1, 1)
            for pair in range(2):
                two = slice(2 * pair, 2 * pair + 2)
                v.wait_ge(s_tot, pair + 1)
                v.tensor_scalar(neg[:, two], bank[2 + pair][:, 0:2], TOPK - 0.5, -1.0, ALU.is_lt,
                                ALU.mult).then_inc(s_add, 1)
                v.wait_ge(s_add, pair + 1)
                v.scalar_tensor_tensor(out=cand[:, two], in0=key[:, two], scalar=biti[:, 0:1], in1=neg[:, two],
                                       op0=ALU.bitwise_or, op1=ALU.bitwise_xor).then_inc(s_cand, 1)

            def decide_bit(e, pair, d, bit):
                two = slice(2 * pair, 2 * pair + 2)
                v.wait_ge(s_tot, e + 1)
                v.tensor_scalar(addb[:, two], bank[2 + pair][:, 0:2], TOPK - 0.5, bitf[:, bass.ds(bit, 1)], ALU.is_ge,
                                ALU.mult).then_inc(s_add, 1)
                v.wait_ge(s_add, d + 1)
                v.tensor_tensor(key[:, two], key[:, two], addb[:, two], ALU.bitwise_or).then_inc(s_key, 1)
                v.wait_ge(s_key, d - 1)
                v.scalar_tensor_tensor(out=cand[:, two], in0=key[:, two], scalar=biti[:, bass.ds(bit + 1, 1)],
                                       in1=neg[:, two], op0=ALU.bitwise_or, op1=ALU.bitwise_xor).then_inc(s_cand, 1)

            def compare_next(e, pair, d, source):
                for j in range(2):
                    v.wait_ge(s_cand, d + 1)
                    v.wait_ge(s_mused, e * 2 + (j - 1))
                    v.tensor_scalar(MASK[:, j, :], source[:, 2 * pair + j, :], candf[:, 2 * pair + j:2 * pair + j + 1],
                                    None, ALU.is_ge).then_inc(s_mask, 1)

            def weight_lo(i, u):
                v.wait_ge(s_whi, i * 2 + (u + 1))
                v.scalar_tensor_tensor(out=HALF[:, u, 1, :], in0=STG[:, u, :], scalar=W_SCALE, in1=HALF[:, u, 0, :],
                                       op0=ALU.mult, op1=ALU.subtract).then_inc(s_wlo, 1)

            v.wait_ge(s_trunc, NT)
            compare_next(2, 0, 2, TRUNC)
            compare_next(3, 1, 2, TRUNC)
            decide_bit(2, 0, 2, 0)
            compare_next(4, 0, 3, TRUNC)
            weight_lo(0, 0)
            weight_lo(0, 1)
            decide_bit(3, 1, 3, 0)
            with v.Fori(0, 7) as i:
                for r in range(2):
                    compare_next(i * 4 + (5 + 2 * r), 1, i * 4 + (4 + 2 * r), TRUNC)
                    decide_bit(i * 4 + (4 + 2 * r), 0, i * 4 + (4 + 2 * r), i * 2 + (1 + r))
                    compare_next(i * 4 + (6 + 2 * r), 0, i * 4 + (5 + 2 * r), TRUNC)
                    weight_lo(i + 1, r)
                    decide_bit(i * 4 + (5 + 2 * r), 1, i * 4 + (5 + 2 * r), i * 2 + (1 + r))
            compare_next(33, 0, 32, ADJ_B)
            with v.Fori(0, 16) as i:
                compare_next(i * 2 + 34, 1, i * 2 + 32, ADJ_B)
                decide_bit(i * 2 + 33, 0, i * 2 + 32, i + 15)
                compare_next(i * 2 + 35, 0, i * 2 + 33, ADJ_B)
                decide_bit(i * 2 + 34, 1, i * 2 + 33, i + 15)
            v.wait_ge(s_cand, 65)
            for b in range(NB):
                for t in range(TC):
                    v.scalar_tensor_tensor(out=X[:, b, t, :], in0=ADJ[:, b, t, :], scalar=candf[:, b:b + 1],
                                           in1=X[:, b, t, :], op0=ALU.is_ge, op1=ALU.add).then_inc(s_x0, 1)
            v.wait_ge(s_x0, NT)
            v.memset(eps[:, :], 1e-6).then_inc(s_ye, 4)

            with v.Fori(0, NB) as b:
                for t in range(TC):
                    v.tensor_copy(XB[:, t, :], X[:, b, t, :]).then_inc(s_xb, 1)
                v.wait_ge(s_std, b + 1)
                v.reciprocal(rstd[:, :], stdx[:, :]).then_inc(s_rstd, 1)
                for c in range(KC + 1):
                    if c < KC:
                        v.wait_ge(s_xT, b * 4 + (c + 1))
                        if c >= 2:
                            v.wait_ge(s_xn, b * 4 + (c - 1))
                        v.tensor_scalar(xnf[:, c % 2, :], bank[2 + c % 2][:, :], mod_a[:, c, bass.ds(b, 1)],
                                        mod_b[:, c, bass.ds(b, 1)], ALU.mult, ALU.add).then_inc(s_xnf, 1)
                    if c:
                        v.wait_ge(s_xnh, b * 4 + c)
                        v.tensor_tensor(XN[:, 1, c - 1, :], xnf[:, (c - 1) % 2, :], XN[:, 0, c - 1, :],
                                        ALU.subtract).then_inc(s_xn, 1)
                for cc in range(9):
                    if cc < 8:
                        v.wait_ge(s_sd, b * 8 + (cc + 1))
                        v.reciprocal(sd[:, cc % 2, :], sd[:, cc % 2, :]).then_inc(s_rr, 1)
                    if cc:
                        v.wait_ge(s_qh, b * 8 + cc)
                        if cc >= 3:
                            v.wait_ge(s_qks[cc - 3], b * 192 + 192)
                        v.tensor_tensor(QKH[:, (cc - 1) % 2, 1, :], qn[:, (cc - 1) % 2, :], QKH[:, (cc - 1) % 2, 0, :],
                                        ALU.subtract).then_inc(s_ql, 1)
                    if cc < 8:
                        v.wait_ge(s_rr, b * 8 + (cc + 1))
                        if cc >= 2:
                            v.wait_ge(s_ql, b * 8 + (cc - 1))
                        v.scalar_tensor_tensor(out=qn[:, cc % 2, :], in0=bank[4 + cc % 2][:, :],
                                               scalar=gqs[:, cc % 2:cc % 2 + 1], in1=sd[:, cc % 2, :],
                                               op0=ALU.mult, op1=ALU.mult).then_inc(s_qn, 1)

                def row_max(h):
                    for t in range(TC):
                        v.wait_ge(s_a, b * 64 + (4 * h + t + 1))
                        v.reduce_max(M16[:, t, 0:1], bank[t % 2][:, :], AX_X).then_inc(s_mx, 1)

                def normalise(h):
                    g32 = slice(32 * (h % 4), 32 * (h % 4) + 32)
                    v.wait_ge(s_av, b * 16 + (h + 1))
                    v.reciprocal(ri[g32, :], bank[6 + h % 2][32:64, :]).then_inc(s_ri, 1)
                    v.wait_ge(s_ri, b * 16 + (h + 1))
                    v.tensor_tensor(OT[g32, h // 4, :], bank[6 + h % 2][0:32, :], ri[g32, :],
                                    ALU.mult).then_inc(s_ao, 1)

                row_max(0)
                for h in range(HEADS + 1):
                    if h:
                        normalise(h - 1)
                    if h + 1 < HEADS:
                        row_max(h + 1)
                for c in range(KC):
                    v.wait_ge(s_oh, b * 4 + (c + 1))
                    v.tensor_tensor(OTH[:, 1, c, :], OT[:, c, :], OTH[:, 0, c, :], ALU.subtract).then_inc(s_ol, 1)
                for n in range(KC + 1):
                    if n < KC:
                        v.wait_ge(s_y, b * 4 + (n + 1))
                        if n >= 2:
                            v.wait_ge(s_x1, b * 4 + (n - 1))
                        v.scalar_tensor_tensor(out=qn[:, n % 2, :], in0=bank[n % 2][:, :], scalar=1.0 / W_SCALE,
                                               in1=OT[:, n, :], op0=ALU.mult, op1=ALU.add).then_inc(s_ye, 1)
                    if n:
                        v.wait_ge(s_ye, b * 4 + (4 + n))
                        v.tensor_tensor(X1V[:, n - 1, b, :], X1V[:, n - 1, b, :], qn[:, (n - 1) % 2, :],
                                        ALU.add).then_inc(s_x1, 1)

            v.memset(ones[:, :], 1.0).then_inc(s_ones, 1)
            v.wait_ge(s_ones, 1)
            for i in range(12):
                v.tensor_scalar(BIASB[:, i, :], ones[:, :], bg24[:, i:i + 1], bg24[:, 12 + i:13 + i] if i < 8 else None,
                                ALU.mult, ALU.add if i < 8 else ALU.bypass)
            for i in range(4):
                v.tensor_scalar(GIc[:, i, :], ones[:, :], bg24[:, 20 + i:21 + i], None, ALU.mult)
            for u in range(2):
                v.memset(dd[:, u, 16:32], EPSILON * ALPHA)
            v.memset(dt6[:, :], DT / 6.0)
            v.memset(X1F[:, T], 0.0)
            v.tensor_copy(zz[0][:, 0:16], cT[:, :])
            v.tensor_copy(zz[0][:, 16:32], cT[:, :])
            v.tensor_copy(hst[:, :], cT[:, :]).then_inc(s_prep, 1)
            v.wait_ge(s_prep, 1)
            v.tensor_copy(QP, cT[:, :]).then_inc(s_q, 1)
            groups(v, scan_group)
            gru_n(T - 1, GB - 1)
            gru_z_half(T - 1, GB - 1)
            gru_z(T - 1)

        @block.gpsimd
        def _(pool):
            def update_h(m):
                pool.wait_ge(s_n, m + 1)
                pool.tensor_tensor(hd[:, :], hst[:, :], ng[:, :], ALU.subtract).then_inc(s_hd, 1)
                pool.wait_ge(s_z, m + 1)
                pool.wait_ge(s_hd, m + 1)
                pool.tensor_tensor(zd[:, :], zs[:, :], hd[:, :], ALU.mult).then_inc(s_zd, 1)
                pool.wait_ge(s_zd, m + 1)
                pool.tensor_tensor(hst[:, :], ng[:, :], zd[:, :], ALU.add).then_inc(s_h, 1)

            def add_h(m):
                pool.wait_ge(s_h, m + 2)
                pool.tensor_tensor(X1F[:, m], X1F[:, m], hst[:, :], ALU.add).then_inc(s_o, 1)

            def sum_drive(n, u):
                pool.tensor_tensor(dd[:, u, 0:16], X1F[:, n], bl2[:, :], ALU.add).then_inc(s_dsum, 1)

            def scale_drive(n, u):
                pool.wait_ge(s_dsum, n + 1)
                pool.tensor_tensor(dd6[:, u, :], dd[:, u, :], dt6[:, :], ALU.mult).then_inc(s_dd, 1)

            def scan_group(g, rk, gi, gru, tail):
                for k in range(GB):
                    n = g * GB + k
                    m = n - LAG * GB
                    after = tail or (gru and k > 0)
                    static = isinstance(n, int)
                    if after:
                        update_h(m - 1)
                        pool.wait_ge(s_h1, m + 1)
                        pool.tensor_tensor(HH[:, :, 1, :], v4(hst[:, :]), HH[:, :, 0, :], ALU.subtract).then_inc(s_h2, 1)
                    x2 = (rk or (k == 0 and gi)) and not (static and n == 0)
                    t = (k - 1) % GB
                    if x2 and not (static and n == 1):
                        pool.wait_ge(s_xl, n - 1)
                    if x2 and k == 1 and not (static and g == 0):
                        pool.wait_ge(s_xg, g)
                    if rk or x2:
                        pool.wait_ge(s_clip, n + 1)
                    if rk:
                        sum_drive(n + 1, (k + 1) % 2)
                    if x2:
                        pool.tensor_tensor(x2f[:, :], X1F[:, n - 1], zc[:, 0:16], ALU.add).then_inc(s_xf, 1)
                        pool.tensor_tensor(XGn[:, :, 0, t, :], v4(X1F[:, n - 1]), v4(zc[:, 0:16]),
                                           ALU.add).then_inc(s_xh, 1)
                    if rk:
                        scale_drive(n + 1, (k + 1) % 2)
                    if x2:
                        pool.wait_ge(s_xf, n)
                        pool.wait_ge(s_xh, n)
                        pool.tensor_tensor(XGn[:, :, 1, t, :], v4(x2f[:, :]), XGn[:, :, 0, t, :],
                                           ALU.subtract).then_inc(s_xl, 1)
                        pool.tensor_tensor(X1F[:, n - 1], X1F[:, n - 1], zc[:, 0:16], ALU.add).then_inc(s_x2, 1)
                        if k == 0:
                            pool.wait_ge(s_xl, n)
                            if not (static and g == 1):
                                pool.wait_ge(s_gim, g * 3 - 3)
                            pool.tensor_tensor(XGc[:, :, :, :, :].rearrange("p c h t b -> p (c h t b)"),
                                               XGn[:, :, :, :, :].rearrange("p c h t b -> p (c h t b)"), ones16[:, :],
                                               ALU.mult).then_inc(s_xg, 1)
                    if after:
                        add_h(m - 1)

            for a in (identf, blk32):
                pool.memset(a[:, :], 0.0 if a is identf else 1.0)
            pool.memset(ones16[:, :], 1.0)
            pool.memset(M16[:, :, :], 0.0)
            for j in range(31):
                pool.memset(bitf[:, j:j + 1], float(2 ** (30 - j)))
            pool.memset(bitf[:, 31:32], 0.0).then_inc(s_bits, 1)
            pool.wait_ge(s_bits, 1)
            pool.affine_select(out=identf[:, :], in_=identf[:, :], compare_op=ALU.not_equal, fill=1.0, base=0,
                               pattern=[[-1, P]], channel_multiplier=1).then_inc(s_iota, 1)
            pool.affine_select(out=blk32[:, :], in_=blk32[:, :], compare_op=ALU.is_ge, fill=0.0, base=0,
                               pattern=[[-32, 4], [0, 32]], channel_multiplier=1).then_inc(s_iota, 1)
            pool.wait_ge(s_iota, 2)
            pool.affine_select(out=blk32[:, :], in_=blk32[:, :], compare_op=ALU.is_ge, fill=0.0, base=31,
                               pattern=[[32, 4], [0, 32]], channel_multiplier=-1)
            pool.tensor_copy(ident16[:, :], identf[:, :]).then_inc(s_const, 1)
            for i in range(NT):
                b, t = i // TC, i % TC
                pool.wait_ge(s_adj, i + 1)
                a = ADJ[:, b, t, t * P:(t + 1) * P]
                pool.affine_select(out=a, in_=a, compare_op=ALU.not_equal, fill=DIAGONAL, base=0,
                                   pattern=[[-1, P]], channel_multiplier=1).then_inc(s_diag, 1)
            pool.wait_ge(s_x0, NT)
            pool.memset(KS[96:128, :, :], -1.0).then_inc(s_kv, 1)
            pool.wait_ge(s_kv, 1)
            pool.memset(V[:, :, :, DH:2 * DH], 1.0).then_inc(s_kv, 1)

            pool.wait_ge(s_prep, 1)
            pool.wait_ge(s_x1, 16)
            pool.wait_ge(s_h1, 1)
            pool.tensor_tensor(HH[:, :, 1, :], v4(hst[:, :]), HH[:, :, 0, :], ALU.subtract).then_inc(s_h2, 1)
            pool.tensor_copy(hd[:, :], hst[:, :]).then_inc(s_h, 1)
            sum_drive(0, 0)
            scale_drive(0, 0)
            groups(pool, scan_group)
            update_h(T - 1)
            add_h(T - 1)

        @block.sync
        def _(sp):
            for b in range(NB):
                sp.dma_start(X[:, b], x[b].rearrange("(t p) d -> p t d", p=P)).then_inc(sx[b], 16)
                if b == 0:
                    sp.dma_start(sideT[:, :], side).then_inc(s_par, 16)
                    sp.dma_start(cT[:, :], condT).then_inc(s_par, 16)
                    sp.dma_start(bemb[:, :], b_emb).then_inc(s_par, 16)
                    sp.dma_start(gn[:, :], g_norm).then_inc(s_par, 16)
                    sp.dma_start(gqk[:, :], g_qk).then_inc(s_par, 16)
                    sp.dma_start(bl2[:, :], bias_l2).then_inc(s_par, 16)
                    sp.dma_start(bg24[:, :], b_gates).then_inc(s_par, 16)
                    sp.dma_start(TB, cond.partition_broadcast(P)).then_inc(s_tb, 16)
            sp.dma_start(WE, W_emb.rearrange("(k p) n -> p k n", p=P)).then_inc(s_we, 16)

            def load_piece(i, u):
                sp.dma_start(STG[:, u, :], W_all[:, bass.ds((i * 2 + u) * W_PIECE, W_PIECE)]).then_inc(s_wld[u], 16)

            def store_piece(i, u):
                sp.wait_ge(s_wlo, i * 2 + (u + 1))
                sp.dma_start(W16F[:, :, bass.ds((i * 2 + u) * W_PIECE, W_PIECE)], HALF[:, u]).then_inc(s_wst[u], 16)

            for u in range(2):
                load_piece(0, u)
            with sp.Fori(0, PIECES // 2 - 1) as i:
                for u in range(2):
                    store_piece(i, u)
                    load_piece(i + 1, u)
            for u in range(2):
                store_piece(PIECES // 2 - 1, u)
            for u in range(2):
                sp.wait_ge(s_wst[u], 16 * PIECES // 2)
            sp.dma_start(W_Q[:, :, :, :], W16[:, :, :, C_QKV:C_OUT]).then_inc(s_wq, 16)
            sp.dma_start(W_O[:, :, :, :], W16[:, :, :, C_OUT:C_IH]).then_inc(s_wq, 16)

            with sp.Fori(0, NB) as b:
                for cc in range(8):
                    stack = (QS, KS)[cc % 2]
                    for half in range(2):
                        sp.wait_ge((s_qh, s_ql)[half], b * 8 + (cc + 1))
                        for r in ((0, 2), (1,))[half] if cc % 2 == 0 else ((0, 1), (2,))[half]:
                            for g in range(4):
                                sp.dma_start(stack[32 * r:32 * r + 32, 4 * (cc // 2) + g, :],
                                             QKH[32 * g:32 * g + 32, cc % 2, half, :]).then_inc(s_qks[cc], 16)

            sp.wait_ge(s_xhat, NT)
            sp.wait_ge(s_xb, NT)
            sp.dma_start(W_CP, W16[:, :, :, C_CPL:C_ALL]).then_inc(s_wl, 16)
            sp.dma_start(W_HH, W16[:, :, :, C_HH:C_CPL]).then_inc(s_wl, 16)
            sp.wait_ge(s_av, NB * HEADS)
            sp.dma_start(W_IH, W16[:, :, :, C_IH:C_HH]).then_inc(s_wl, 16)
            with sp.Fori(0, NG) as j:
                sp.wait_ge(s_o, j * GB + GB)
                sp.dma_start(out[:, bass.ds(j * GB, GB), :], X1F[:, bass.ds(j * GB, GB), :]).then_inc(s_out, 16)
            sp.wait_ge(s_out, 16 * NG)


_ORDER = ["x", "side", "condT", "cond", "W_emb", "b_emb", "g_norm", "g_qk", "W_all", "bias_l2", "b_gates"]


def kernel(x, fside_BxSx1_0, cond_2048, L1_cond_W_emb, L1_cond_b_emb, L1_cond_g_norm, L1_cond_W_qkv, L1_cond_g_q,
           L1_cond_g_k, L1_cond_W_out, L2_cond_coupling, L2_cond_bias, L3_cond_W_ih, L3_cond_W_hh, L3_cond_b_ih,
           L3_cond_b_hh):
    import numpy as np
    import concourse.bacc as bacc
    from concourse.bass_utils import run_bass_kernel_spmd

    def columns(a):
        return np.asarray(a).reshape(-1, P).T

    cond = np.asarray(cond_2048)
    w_all = np.concatenate([np.asarray(L1_cond_W_qkv), np.asarray(L1_cond_W_out), np.asarray(L3_cond_W_ih),
                            np.asarray(L3_cond_W_hh), np.asarray(L2_cond_coupling).T], axis=1)
    arrays = {
        "x": np.asarray(x),
        "side": np.asarray(fside_BxSx1_0).reshape(NB * TC, P).T,
        "condT": cond.reshape(NB, KC, P).transpose(2, 1, 0).reshape(P, S16),
        "cond": cond,
        "W_emb": np.asarray(L1_cond_W_emb),
        "b_emb": columns(L1_cond_b_emb),
        "g_norm": columns(L1_cond_g_norm),
        "g_qk": np.stack([np.tile(np.asarray(L1_cond_g_q), P // DH), np.tile(np.asarray(L1_cond_g_k), P // DH)], axis=1),
        "W_all": w_all.reshape(KC, P, C_ALL).transpose(1, 0, 2).reshape(P, KC * C_ALL),
        "bias_l2": np.repeat(columns(L2_cond_bias), NB, axis=1),
        "b_gates": np.concatenate([columns(L3_cond_b_ih), columns(L3_cond_b_hh)], axis=1),
    }
    arrays = {k: np.ascontiguousarray(a) for k, a in arrays.items()}
    nc = bacc.Bacc("TRN2", target_bir_lowering=False, num_devices=1)
    args = [nc.dram_tensor(f"in_{k}", arrays[k].shape, mybir.dt.from_np(arrays[k].dtype), kind="ExternalInput").ap()
            for k in _ORDER]
    out = nc.dram_tensor("out_x", (P, T, S16), F32, kind="ExternalOutput").ap()
    mixed_scan_kernel(nc, *args, out)
    r = run_bass_kernel_spmd(nc, [{f"in_{k}": a for k, a in arrays.items()}], core_ids=[0])
    got = np.asarray(r.results[0]["out_x"]).reshape(P, T, KC, NB)
    return np.ascontiguousarray(got.transpose(3, 1, 2, 0).reshape(NB, T, D))
```

```python
from contextlib import ExitStack

import concourse.bass as bass
from concourse import mybir

F32 = mybir.dt.float32
F16 = mybir.dt.float16
BF16 = mybir.dt.bfloat16
I32 = mybir.dt.int32
ALU = mybir.AluOpType
ACT = mybir.ActivationFunctionType
AX_X = mybir.AxisListType.X

P = 128
NB, T, D = 4, 512, 512
KC = D // P
TC = T // P
NT = NB * TC
S16 = KC * NB
HEADS, DH = 16, 32
TOPK = 5120
DIAGONAL = -3.0e38
C_QKV, C_OUT, C_IH, C_HH, C_CPL, C_ALL = 0, 1536, 2048, 3584, 5120, 5632
W_PIECE = C_ALL // 4

DT, EPSILON, ALPHA, BETA, CLAMP = 0.01, 0.08, 0.7, 0.8, 20.0
C_STAGE = [0.5 * DT, 0.5 * DT, DT, DT / 6.0]
W_SCALE = 128.0
GB = 4
NG = T // GB
LAG = 2
GH_CUT = [0, 0, 32, 64, 96]
GI_CUT = [0] + [96 * k // (GB - 1) for k in range(GB)]
EVACUATE = [(2, 1), (3, 1), (3, 2)]
PRE = 19


def mixed_scan_kernel(nc, x, side, condT, cond, W_emb, b_emb, g_norm, g_qk, W_all, bias_l2, b_gates, out):
    ctx = ExitStack()
    with ctx:
        def sb(name, shape, dt=F32):
            return ctx.enter_context(nc.sbuf_tensor(name, shape, dt))

        def sem(name):
            return ctx.enter_context(nc.semaphore(name))

        bank = [ctx.enter_context(nc.psum_tensor(f"bank{i}", [P, 512], F32)) for i in range(8)]

        R_X = sb("R_X", [P, 8192])
        R_A = sb("R_A", [P, 12288])
        R_B = sb("R_B", [P, 4096])
        R_T = sb("R_T", [P, (T + 1) * S16])
        R_H = sb("R_H", [P, 6144])
        W_Q = sb("W_Q", [P, 2, KC, 1536], F16)
        W_O = sb("W_O", [P, 2, KC, 512], F16)

        X = R_X[:, :].rearrange("p (b t d) -> p b t d", b=NB, t=TC)
        ADJ = R_A[:, 0:8192].rearrange("p (b t d) -> p b t d", b=NB, t=TC)
        ADJ_B = R_A[:, 0:8192].rearrange("p (b n) -> p b n", b=NB)
        TRUNC = R_A[:, 8192:12288].bitcast(BF16).rearrange("p (b n) -> p b n", b=NB)
        MASK = R_B[:, 0:2048].bitcast(F16).rearrange("p (u n) -> p u n", u=2)
        TB = R_B[:, 2048:4096].rearrange("p (b d) -> p b d", b=NB)
        STG = R_T[:, 0:2 * W_PIECE].rearrange("p (u n) -> p u n", u=2)
        HALF = R_T[:, 2 * W_PIECE:4 * W_PIECE].bitcast(F16).rearrange("p (u h n) -> p u h n", u=2, h=2)
        W_SCALES = R_T[:, 4 * W_PIECE:5 * W_PIECE]
        WE = R_H[:, 0:4096].rearrange("p (k n) -> p k n", k=KC)
        X1T = R_T[:, 0:T * 16].rearrange("p (t c b) -> p t c b", t=T, c=KC)
        X1F = R_T[:, 0:(T + 1) * 16].rearrange("p (t s) -> p t s", t=T + 1)
        W_HH = R_X[:, 0:6144].bitcast(F16).rearrange("p (h k n) -> p h k n", h=2, k=KC)
        W_CP = R_X[:, 6144:8192].bitcast(F16).rearrange("p (h k n) -> p h k n", h=2, k=KC)
        W_IH = R_A[:, 0:6144].bitcast(F16).rearrange("p (h k n) -> p h k n", h=2, k=KC)

        W16 = nc.dram_tensor("w16_scratch", (P, 2, KC, C_ALL), F16, kind="Internal").ap()
        QKD = nc.dram_tensor("qk_scratch", (8, 2, P, T), F16, kind="Internal").ap()
        W16F = W16.rearrange("p h k n -> p h (k n)")
        XN = R_H[:, 0:2048].bitcast(F16).rearrange("p (h k n) -> p h k n", h=2, k=KC)
        OTH = XN
        OT = R_H[:, 2048:4096].rearrange("p (c n) -> p c n", c=KC)
        XB = OT
        QKH = R_H[:, 4096:5120].bitcast(F16).rearrange("p (u h n) -> p u h n", u=2, h=2)
        xnf = R_H[:, 5120:6144].rearrange("p (u n) -> p u n", u=2)
        XH = R_B[:, 0:2048].rearrange("p (t d) -> p t d", t=TC)
        PT = R_B[:, :].rearrange("p (u k n) -> p u k n", u=2, k=KC)
        QS = R_A[:, 0:4096].bitcast(F16).rearrange("p (h n) -> p h n", h=HEADS)
        KS = R_A[:, 4096:8192].bitcast(F16).rearrange("p (h n) -> p h n", h=HEADS)
        V = R_A[:, 8192:12288].rearrange("p (t h e) -> p t h e", t=TC, h=HEADS)
        X1V = R_T[:, 0:T * S16].rearrange("p (t c b) -> p c b t", t=T, c=KC)
        sqf = sb("sqf", [P, 2, 512])
        sd = sb("sd", [P, 2, 512])
        qn = sb("qn", [P, 2, 512])
        identf = sb("identf", [P, P])
        blk32 = sb("blk32", [P, P])
        ident16 = sb("ident16", [P, P], F16)
        ones16 = sb("ones16", [P, 2 * KC * GB * NB], F16)
        M16 = sb("M16", [P, 2, TC, 32], F16)
        sideT = sb("sideT", [P, NT])
        bemb = sb("bemb", [P, 8])
        gn = sb("gn", [P, KC])
        gqk = sb("gqk", [P, 2])
        gqs = sb("gqs", [P, 2])
        mod_a = sb("mod_a", [P, KC, NB])
        mod_b = sb("mod_b", [P, KC, NB])
        nmx = sb("nmx", [P, NT])
        esum = sb("esum", [P, NT])
        rsum = sb("rsum", [P, NT])
        rsc = sb("rsc", [P, NT])
        bitf = sb("bitf", [P, 32])
        biti = sb("biti", [P, 32], I32)
        key = sb("key", [P, NB], I32)
        zero = sb("zero", [P, NB], I32)
        cand = sb("cand", [P, NB], I32)
        addb = sb("addb", [P, NB], I32)
        c16 = sb("c16", [P, NB], F16)
        ssx = sb("ssx", [P, NT])
        stdx = sb("stdx", [P, NT])
        rstd = sb("rstd", [P, NT])
        eps = sb("eps", [P, 1])
        candf = cand[:, :].bitcast(F32)

        sx = [sem(f"x_loaded_{b}") for b in range(NB)]
        s_par = sem("small_loaded")
        s_we = sem("w_emb_loaded")
        s_tb = sem("cond_loaded")
        s_const = sem("constants_ready")
        s_iota = sem("identity_steps")
        s_max = sem("score_max")
        s_exp = sem("score_exp")
        s_rs = sem("score_scales")
        s_adj = sem("scores_ready")
        s_diag = sem("diagonal_out")
        s_trunc = sem("scores_truncated")
        s_mask = sem("mask_ready")
        s_mused = sem("mask_counted")
        s_c16 = sem("counts_copied")
        s_tot = sem("totals_ready")
        s_add = sem("bit_decided")
        s_key = sem("key_ready")
        s_cand = sem("candidate_ready")
        s_bits = sem("bit_table")
        s_wld = [sem(f"piece_loaded_{u}") for u in range(2)]
        s_whi = sem("piece_hi")
        s_wsc = sem("piece_scaled")
        s_wlo = sem("piece_lo")
        s_wst = [sem(f"piece_stored_{u}") for u in range(2)]
        s_wq = sem("projection_weights")
        s_emb = sem("scale_shift_done")
        s_modt = sem("modulation_steps")
        s_x0 = sem("x0_ready")
        s_kv = sem("key_value_constants")
        s_xb = sem("x_rows_copied")
        s_ss = sem("row_squares")
        s_std = sem("row_std")
        s_rstd = sem("row_rstd")
        s_xhat = sem("x_hat")
        s_raw = sem("x_transposed")
        s_rawE = sem("x_transposed_out")
        s_xT = sem("x_hat_transposed")
        s_xnf = sem("x_normed")
        s_xnh = sem("x_normed_hi")
        s_xn = sem("x_normed_halves")
        s_qk = sem("qk_projected")
        s_sqf = sem("qk_squared")
        s_ssq = sem("qk_squares_summed")
        s_sd = sem("qk_std")
        s_rr = sem("qk_rstd")
        s_qn = sem("qk_normed")
        s_qh = sem("qk_hi")
        s_ql = sem("qk_lo")
        s_qks = [sem(f"qk_stacked_{c}") for c in range(8)]
        s_qst = [sem(f"qk_stored_{u}") for u in range(2)]
        s_v = sem("v_projected")
        s_ve = sem("v_ready")
        s_a = sem("logits_rows")
        s_mx = sem("row_max")
        s_mt = sem("max_transposed")
        s_mc = sem("max_stacked")
        s_st = sem("logits_columns")
        s_e = sem("attention_weights")
        s_av = sem("values_summed")
        s_oe = sem("values_sums_read")
        s_ri = sem("softmax_sums")
        s_ao = sem("attention_out")
        s_oh = sem("attention_hi")
        s_ol = sem("attention_lo")
        s_y = sem("out_projected")
        s_ye = sem("out_projection_read")
        s_x1 = sem("x1_ready")

        cT = sb("cT", [P, S16])
        bl2 = sb("bl2", [P, S16])
        bg24 = sb("bg24", [P, 24])
        BIASB = sb("BIASB", [P, 12, GB * NB])
        ones = sb("ones", [P, GB * NB])

        TT = sb("TT", [P, KC, 2, NB], F16)
        HH = sb("HH", [P, KC, 2, NB], F16)
        tf = sb("tf", [P, S16])
        sq = sb("sq", [P, S16])
        zc = sb("zc", [P, 32])
        dd = sb("dd", [P, 2, 32])
        dt6 = sb("dt6", [P, 32])
        x2f = sb("x2f", [P, S16])
        dd6 = sb("dd6", [P, 2, 32])
        wa = sb("wa", [P, 32])
        wb = sb("wb", [P, 32])
        w4 = sb("w4", [P, 32])
        e1 = sb("e1", [P, 32])
        e2 = sb("e2", [P, 32])
        e3 = sb("e3", [P, 32])
        gq = sb("gq", [P, S16])
        gp = sb("gp", [P, S16])
        ncub = sb("ncub", [P, S16])
        base = sb("base", [P, S16])
        part = sb("part", [P, S16])
        XGn = sb("XGn", [P, KC, 2, GB, NB], F16)
        XGc = sb("XGc", [P, KC, 2, GB, NB], F16)
        gie = sb("gie", [P, 2, 4, GB * NB])
        GIn = sd[:, 1, 0:12 * GB * NB].rearrange("p (n c) -> p n c", n=12)
        GIc = sd[:, 0, 0:16 * GB * NB].rearrange("p (n c) -> p n c", n=16)
        nr1 = sb("nr1", [P, 32])
        nr = sb("nr", [P, 32])
        zg1 = sb("zg1", [P, S16])
        zg = sb("zg", [P, S16])
        rg = sb("rg", [P, S16])
        zs = sb("zs", [P, S16])
        rn = sb("rn", [P, S16])
        npre = sb("npre", [P, S16])
        ng = sb("ng", [P, S16])
        hd = sb("hd", [P, S16])
        zd = sb("zd", [P, S16])
        hst = sb("hst", [P, S16])

        Z = sb("Z", [P, 128])
        QP = bank[0][:, 0:S16]
        zz = [Z[:, 32 * s:32 * s + 32] for s in range(4)]
        qq = [Z[:, 32 * s:32 * s + 16] for s in range(4)]
        pp = [Z[:, 32 * s + 16:32 * s + 32] for s in range(4)]
        CPL = bank[1][:, 0:32].rearrange("p (h j b) -> p h j b", h=2, j=KC)
        GHN = bank[2][:, 0:64].rearrange("p (h n b) -> p h n b", h=2, n=8)
        GHZ = bank[5][:, 0:32].rearrange("p (h n b) -> p h n b", h=2, n=4)
        GI = [bank[i][:, 0:8 * GB * NB].rearrange("p (n h c) -> p n h c", n=4, h=2) for i in (3, 4, 6)]


        def v4(a):
            return a.rearrange("p (c b) -> p c b", b=NB)

        s_prep = sem("scan_params_ready")
        s_wl = sem("scan_weights_loaded")
        s_q = sem("q_ready")
        s_qs = sem("q_stored")
        s_t1 = sem("tanh_hi_ready")
        s_tf = sem("tanh_ready")
        s_sq = sem("square_ready")
        s_t2 = sem("tanh_lo_ready")
        s_cp = sem("couple_ready")
        s_pre = sem("vec_pre")
        s_clip = sem("state_clipped")
        s_dd = sem("drive_ready")
        s_dsum = sem("drive_summed")
        s_x2 = sem("x2_ready")
        s_xf = sem("x2_full_ready")
        s_xh = sem("x2_hi_ready")
        s_xl = sem("x2_lo_ready")
        s_xg = sem("x2_group_ready")
        s_gim = sem("gi_matmuls_done")
        s_gie = sem("gi_half_summed")
        s_gin = sem("gi_next_ready")
        s_gic = sem("gi_current_ready")
        s_ghnr = sem("gh_nr_done")
        s_ghz = sem("gh_z_done")
        s_ones = sem("ones_ready")
        s_nr1 = sem("nr_half")
        s_nr = sem("nr_ready")
        s_r = sem("r_ready")
        s_rn = sem("rn_ready")
        s_np = sem("n_pre_ready")
        s_n = sem("n_ready")
        s_zg1 = sem("z_half")
        s_zg = sem("z_pre_ready")
        s_z = sem("z_ready")
        s_hd = sem("h_minus_n")
        s_zd = sem("z_h_minus_n")
        s_h = sem("h_ready")
        s_h1 = sem("h_hi_ready")
        s_h2 = sem("h_lo_ready")
        s_o = sem("out_ready")
        s_out = sem("out_written")

        GH_MM = [(half, k, wblk + j, slot + j)
                 for slot, wblk in ((0, 8), (4, 0), (8, 4)) for half in (1, 0) for j in range(4) for k in range(KC)]
        GI_MM = [(half, k, wblk + j) for wblk in (0, 4, 8) for j in range(4) for half in (1, 0) for k in range(KC)]

        def groups(eng, body):
            for g in range(4):
                body(g, True, g >= 1, g >= LAG, g > LAG)
            with eng.Fori(0, (NG - 4) // 4) as i:
                for u in range(4):
                    body(i * 4 + (4 + u), True, True, True, True)
            body(NG, False, True, True, True)
            body(NG + 1, False, False, True, True)

        SPLIT_MM = [(hw, hx, c) for hw, hx in ((0, 0), (0, 1), (1, 0)) for c in range(KC)]
        ST_BANK = [2, 3, 4]
        PROJ_BANK = [0, 1, 5, 2]
        PIECES = 4 * KC

        block = ctx.enter_context(nc.Block())

        @block.tensor
        def _(pe):
            def scan_group(g, rk, gi, gru, tail):
                for k in range(GB):
                    n = g * GB + k
                    m = n - LAG * GB
                    for s in range(4):
                        if rk:
                            pe.wait_ge(s_t1, n * 4 + (s + 1))
                            if not (isinstance(n, int) and n == 0 and s == 0):
                                pe.wait_ge(s_qs, n * 4 + s)
                            for j in range(KC):
                                for c in range(KC):
                                    pe.matmul(CPL[:, 0, j, :], W_CP[:, 1, c, j * P:(j + 1) * P], TT[:, c, 0, :],
                                              start=(j == 0 and c == 0), stop=False, skip_group_check=True)
                            pe.wait_ge(s_t2, n * 4 + (s + 1))
                            for j in range(KC):
                                for c in range(KC):
                                    mm = pe.matmul(CPL[:, :, j, :], W_CP[:, 0, c, j * P:(j + 1) * P], TT[:, c, :, :],
                                                   start=False, stop=(c == KC - 1), skip_group_check=True)
                            mm.then_inc(s_cp, 1)
                        if gi and s == 0 and k:
                            if k == 1:
                                pe.wait_ge(s_xg, g)
                                if tail or gru:
                                    pe.wait_ge(s_gin, g * 3 - 3)
                            for i in range(GI_CUT[k], GI_CUT[k + 1]):
                                half, c, blk = GI_MM[i]
                                o = GI[blk // 4][:, blk % 4]
                                if half:
                                    mm = pe.matmul(o[:, 0, :], W_IH[:, 1, c, blk * P:(blk + 1) * P], XGc[:, c, 0],
                                                   start=(blk % 4 == 0 and c == 0), stop=False, skip_group_check=True)
                                else:
                                    mm = pe.matmul(o, W_IH[:, 0, c, blk * P:(blk + 1) * P], XGc[:, c],
                                                   start=False, stop=(c == KC - 1), skip_group_check=True)
                                if i % 32 == 31:
                                    mm.then_inc(s_gim, 1)
                        if gru:
                            for i in range(GH_CUT[s], GH_CUT[s + 1]):
                                half, c, wblk, slot = GH_MM[i]
                                if i == 0:
                                    pe.wait_ge(s_h1, m + 1)
                                if i == 16:
                                    pe.wait_ge(s_h2, m + 1)
                                o = GHN[:, :, slot] if slot < 8 else GHZ[:, :, slot - 8]
                                if half:
                                    mm = pe.matmul(o[:, 0], W_HH[:, 1, c, wblk * P:(wblk + 1) * P], HH[:, c, 0],
                                                   start=(i in (0, 64)), stop=False, skip_group_check=True)
                                else:
                                    mm = pe.matmul(o, W_HH[:, 0, c, wblk * P:(wblk + 1) * P], HH[:, c],
                                                   start=False, stop=(c == KC - 1), skip_group_check=True)
                                if i == 63:
                                    mm.then_inc(s_ghnr, 1)
                                if i == 95:
                                    mm.then_inc(s_ghz, 1)

            pe.wait_ge(s_par, 16 * 7)
            pe.wait_ge(s_we, 16)
            for n in range(8):
                for c in range(KC):
                    mm = pe.matmul(bank[4][:, n * NB:(n + 1) * NB], WE[:, c, n * P:(n + 1) * P],
                                   cT[:, c * NB:(c + 1) * NB], start=(c == 0), stop=(c == KC - 1))
            mm.then_inc(s_emb, 1)

            def count(e, pair, after_unread=False):
                for j in range(2):
                    pe.wait_ge(s_mask, e * 2 + (j + 1))
                    if j == 0 and after_unread:
                        pe.wait_ge(s_c16, e)
                    for t in range(16):
                        mm = pe.matmul(bank[pair][:, j:j + 1], MASK[:, j, t * P:(t + 1) * P], ones16[:, 0:1],
                                       start=(t == 0), stop=(t == 15))
                    mm.then_inc(s_mused, 1)
                pe.wait_ge(s_mused, e * 2 + 2)
                pe.wait_ge(s_c16, e + 1)
                pe.matmul(bank[2 + pair][:, 0:2], ones16[:, 0:P], c16[:, 2 * pair:2 * pair + 2],
                          start=True, stop=True).then_inc(s_tot, 1)

            pe.wait_ge(s_const, 1)
            count(0, 0)
            count(1, 1)
            count(2, 0)
            count(3, 1)
            count(4, 0)
            with pe.Fori(0, 14) as i:
                count(i * 2 + 5, 1)
                count(i * 2 + 6, 0)
            count(33, 0, True)
            with pe.Fori(0, 16) as i:
                count(i * 2 + 34, 1)
                count(i * 2 + 35, 0)

            pe.wait_ge(s_wq, 32)
            pe.wait_ge(s_kv, 2)
            with pe.Fori(0, NB) as b:
                for src, first, ready, read, done in ((XH, 3, s_xhat, s_xnf, s_xT), (XB, 6, s_xb, s_rawE, s_raw)):
                    pe.wait_ge(ready, b * 4 + 4)
                    for c in range(KC):
                        if c >= 2:
                            pe.wait_ge(read, b * 4 + (c - 1))
                        for t in range(TC):
                            mm = pe.transpose(bank[first + c % 2][:, t * P:(t + 1) * P], src[:, t, c * P:(c + 1) * P],
                                              identf[:, :])
                        mm.then_inc(done, 1)

                def square_sum(cc):
                    pe.wait_ge(s_sqf, b * 8 + (cc + 1))
                    if cc < 2:
                        pe.wait_ge(s_rawE, b * 4 + 4)
                    else:
                        pe.wait_ge(s_sd, b * 8 + (cc - 1))
                    pe.matmul(bank[6 + cc % 2][:, :], blk32[:, :], sqf[:, cc % 2, :],
                              start=True, stop=True).then_inc(s_ssq, 1)

                def project_v(t):
                    if t < 2:
                        pe.wait_ge(s_xnf, b * 4 + 4)
                    else:
                        pe.wait_ge(s_ve, b * 4 + (t - 1))
                    for i, (hw, hx, c) in enumerate(SPLIT_MM):
                        mm = pe.matmul(bank[3 + t % 2][:, :], XN[:, hx, c, t * P:(t + 1) * P], W_Q[:, hw, c, 1024:1536],
                                       start=(i == 0), stop=(i == 11))
                    mm.then_inc(s_v, 1)

                pe.wait_ge(s_xn, b * 4 + 4)
                for cc in range(8):
                    if cc < 4:
                        pe.wait_ge(s_ye, b * 4 + (cc + 1))
                    else:
                        pe.wait_ge(s_qn, b * 8 + (cc - 3))
                    col = 512 * (cc % 2) + P * (cc // 2)
                    for i, (hw, hx, c) in enumerate(SPLIT_MM):
                        mm = pe.matmul(bank[PROJ_BANK[cc % 4]][:, :], W_Q[:, hw, c, col:col + P], XN[:, hx, c, :],
                                       start=(i == 0), stop=(i == 11))
                    mm.then_inc(s_qk, 1)
                    if cc:
                        square_sum(cc - 1)
                    if cc >= 3 and cc < 7:
                        project_v(cc - 3)
                square_sum(7)

                def logits_rows(h, t):
                    if h % 4 == 0 and t == 0:
                        pe.wait_ge(s_qks[h // 2], b * 48 + 48)
                        pe.wait_ge(s_qks[h // 2 + 1], b * 48 + 48)
                    if h == 0 and t < 2:
                        pe.wait_ge(s_qn, b * 8 + (5 + t))
                    else:
                        pe.wait_ge(s_mx, b * 64 + (4 * h + t - 1))
                    pe.matmul(bank[t % 2][:, :], QS[0:96, h, t * P:(t + 1) * P], KS[0:96, h, :],
                              start=True, stop=True).then_inc(s_a, 1)

                def max_to_row(h):
                    pe.wait_ge(s_mx, b * 64 + (4 * h + 4))
                    if h == 0:
                        pe.wait_ge(s_qn, b * 8 + 7)
                    else:
                        pe.wait_ge(s_mc, b * 16 + h)
                    for t in range(TC):
                        mm = pe.transpose(bank[5][96:128, :].bitcast(F16)[:, t * P:(t + 1) * P], M16[:, h % 2, t, :],
                                          ident16[:, :])
                    mm.then_inc(s_mt, 1)

                def logits_columns(h, t):
                    n = 4 * h + t
                    if t == 0:
                        pe.wait_ge(s_mc, b * 16 + (h + 1))
                    if n == 0:
                        pe.wait_ge(s_qn, b * 8 + 8)
                    elif n < 3:
                        pe.wait_ge(s_ve, b * 4 + 4)
                    else:
                        pe.wait_ge(s_e, b * 64 + (n - 2))
                    pe.matmul(bank[ST_BANK[n % 3]][:, :], KS[:, h, t * P:(t + 1) * P], QS[:, h, :],
                              start=True, stop=True).then_inc(s_st, 1)

                def sum_values(h, t):
                    if t == 0:
                        if h < 2:
                            pe.wait_ge(s_sd, b * 8 + 8)
                            pe.wait_ge(s_ve, b * 4 + 4)
                        else:
                            pe.wait_ge(s_oe, b * 16 + (h - 1))
                    pe.wait_ge(s_e, b * 64 + (4 * h + t + 1))
                    mm = pe.matmul(bank[6 + h % 2][0:64, :], V[:, t, h, :], PT[:, h % 2, t, :],
                                   start=(t == 0), stop=(t == 3))
                    if t == 3:
                        mm.then_inc(s_av, 1)

                for t in range(TC):
                    logits_rows(0, t)
                for h in range(HEADS + 1):
                    for t in range(TC):
                        if h:
                            sum_values(h - 1, t)
                        if h + 1 < HEADS:
                            logits_rows(h + 1, t)
                        if h < HEADS:
                            if t == 0:
                                max_to_row(h)
                            if t == 1:
                                logits_columns(h, 0)
                            if t:
                                logits_columns(h, t)

                for cs in (range(KC - 1), range(KC - 1, KC)):
                    pe.wait_ge(s_ol, b * 4 + (cs[-1] + 1))
                    for n in range(KC):
                        if cs[0] == 0 and n == 0:
                            pe.wait_ge(s_mx, b * 64 + 64)
                        if cs[0] == 0 and n == 2:
                            pe.wait_ge(s_mc, b * 16 + 16)
                        for c in cs:
                            for hw, hx in ((0, 0), (0, 1), (1, 0)):
                                mm = pe.matmul(bank[PROJ_BANK[n]][:, :], W_O[:, hw, c, n * P:(n + 1) * P],
                                               OTH[:, hx, c, :], start=(c == 0 and hw == 0 and hx == 0),
                                               stop=(c == KC - 1 and hw == 1))
                        if cs[-1] == KC - 1:
                            mm.then_inc(s_y, 1)

            pe.wait_ge(s_wl, 48)
            groups(pe, scan_group)

        @block.scalar
        def _(act):
            def truncate(i):
                b, t = i // TC, i % TC
                act.wait_ge(s_diag, i + 1)
                act.activation(TRUNC[:, b, t * D:(t + 1) * D],
                               ADJ[:, b, t, :].bitcast(BF16).rearrange("p (n e) -> p e n", e=2)[:, 1, :],
                               ACT.Copy).then_inc(s_trunc, 1)

            def scan_group(g, rk, gi, gru, tail):
                for k in range(GB):
                    n = g * GB + k
                    m = n - LAG * GB
                    after = tail or (gru and k > 0)
                    for s in range(4):
                        if rk:
                            act.wait_ge(s_q, n * 4 + (s + 1))
                            act.activation(TT[:, :, 0, :], v4(QP), ACT.Tanh).then_inc(s_t1, 1)
                            act.activation(tf[:, :], QP, ACT.Tanh).then_inc(s_tf, 1)
                            if s == 0:
                                act.wait_ge(s_clip, n + 1)
                            act.activation(sq[:, :], zc[:, 0:16] if s == 0 else QP, ACT.Square,
                                           scale=(C_STAGE[s] / 3.0) ** 0.5).then_inc(s_sq, 1)
                        if gru and k == 0 and s == 1:
                            act.wait_ge(s_gin, g * 3 - 3)
                            if tail:
                                act.wait_ge(s_zg, m)
                            act.activation(GIc[:, 4:16, :], GIn[:, :, :], ACT.Copy).then_inc(s_gic, 1)
                        if after and s == 0:
                            act.wait_ge(s_np, m)
                            act.activation(ng[:, :], npre[:, :], ACT.Tanh).then_inc(s_n, 1)
                            act.wait_ge(s_zg, m)
                            act.activation(zs[:, :], zg[:, :], ACT.Sigmoid).then_inc(s_z, 1)
                        if after and s == 1:
                            act.wait_ge(s_h, m + 1)
                            act.activation(HH[:, :, 0, :], v4(hst[:, :]), ACT.Copy).then_inc(s_h1, 1)
                        if gru and s == 3:
                            act.wait_ge(s_nr, m + 1)
                            act.activation(rg[:, :], nr[:, 16:32], ACT.Sigmoid).then_inc(s_r, 1)

            for i in range(NT):
                b, t = i // TC, i % TC
                act.wait_ge(s_max, i + 1)
                act.activation(ADJ[:, b, t, :], X[:, b, t, :], ACT.Exp, bias=nmx[:, i:i + 1],
                               accum_out=esum[:, i:i + 1]).then_inc(s_exp, 1)
                if i >= 6:
                    truncate(i - 6)
            for i in range(NT - 6, NT):
                truncate(i)

            def copy_counts(e, pair):
                act.wait_ge(s_mused, e * 2 + 2)
                act.activation(c16[:, 2 * pair:2 * pair + 2], bank[pair][:, 0:2], ACT.Copy).then_inc(s_c16, 1)

            def weight_hi(i, u, first=False):
                act.wait_ge(s_wld[u], i * 16 + 16)
                if not first:
                    act.wait_ge(s_wst[u], i * 16)
                act.activation(HALF[:, u, 0, :], STG[:, u, :], ACT.Copy, scale=W_SCALE).then_inc(s_whi, 1)

            for e in range(2):
                copy_counts(e, e % 2)
            for u in range(2):
                weight_hi(0, u, True)
            for e in range(2, 5):
                copy_counts(e, e % 2)
            with act.Fori(0, 14) as i:
                copy_counts(i * 2 + 5, 1)
                copy_counts(i * 2 + 6, 0)
            copy_counts(33, 0)
            with act.Fori(0, 7) as i:
                for u in range(2):
                    copy_counts(i * 4 + (34 + 2 * u), 1)
                    copy_counts(i * 4 + (35 + 2 * u), 0)
                    weight_hi(i + 1, u)
            for e in range(62, 66):
                copy_counts(e, (e + 1) % 2)

            for i in range(NT):
                act.wait_ge(s_x0, i + 1)
                if i >= 8:
                    act.wait_ge(s_ss, i - 7)
                act.activation(PT[:, i // 4 % 2, i % 4, :], X[:, i // TC, i % TC, :], ACT.Square,
                               accum_out=ssx[:, i:i + 1]).then_inc(s_ss, 1)
            act.wait_ge(s_ss, NT)
            act.wait_ge(s_ye, 4)
            act.activation(stdx[:, :], ssx[:, :], ACT.Sqrt, bias=eps[:, 0:1], scale=1.0 / D).then_inc(s_std, 1)
            act.wait_ge(s_rstd, 1)
            with act.Fori(0, NB) as b:
                for t in range(TC):
                    act.activation(XH[:, t, :], X[:, b, t, :], ACT.Copy,
                                   scale=rstd[:, bass.ds(b * TC + t, 1)]).then_inc(s_xhat, 1)
                for c in range(KC):
                    act.wait_ge(s_xnf, b * 4 + (c + 1))
                    act.activation(XN[:, 0, c, :], xnf[:, c % 2, :], ACT.Copy).then_inc(s_xnh, 1)
                for c in range(KC):
                    act.wait_ge(s_raw, b * 4 + (c + 1))
                    act.activation(X1V[:, c, b, :], bank[6 + c % 2][:, :], ACT.Copy).then_inc(s_rawE, 1)
                for cc in range(10):
                    if cc < 8:
                        act.wait_ge(s_qk, b * 8 + (cc + 1))
                        if cc >= 2:
                            act.wait_ge(s_ssq, b * 8 + (cc - 1))
                        act.activation(sqf[:, cc % 2, :], bank[PROJ_BANK[cc % 4]][:, :], ACT.Square,
                                       scale=1.0 / W_SCALE).then_inc(s_sqf, 1)
                    if 1 <= cc <= 8:
                        act.wait_ge(s_ssq, b * 8 + cc)
                        if cc >= 3:
                            act.wait_ge(s_qn, b * 8 + (cc - 2))
                        act.activation(sd[:, (cc - 1) % 2, :], bank[6 + (cc - 1) % 2][:, :], ACT.Sqrt,
                                       bias=eps[:, 0:1], scale=1.0 / DH).then_inc(s_sd, 1)
                    if cc >= 2:
                        act.wait_ge(s_qn, b * 8 + (cc - 1))
                        if cc >= 4:
                            act.wait_ge(s_qst[cc % 2], b * 128 + (cc // 2 - 1) * 32)
                        act.activation(QKH[:, cc % 2, 0, :], qn[:, cc % 2, :], ACT.Copy).then_inc(s_qh, 1)
                    if 4 <= cc < 8:
                        t = cc - 4
                        act.wait_ge(s_v, b * 4 + (t + 1))
                        act.activation(V[:, t, :, 0:DH], bank[3 + t % 2][:, :].rearrange("p (h d) -> p h d", h=HEADS),
                                       ACT.Copy, scale=1.0 / W_SCALE).then_inc(s_ve, 1)

                def attention_hi(c):
                    act.wait_ge(s_ao, b * 4 + (c + 1))
                    act.activation(OTH[:, 0, c, :], OT[:, c, :], ACT.Copy).then_inc(s_oh, 1)

                def read_values(h):
                    g32 = slice(32 * (h % 4), 32 * (h % 4) + 32)
                    act.wait_ge(s_av, b * 16 + (h + 1))
                    if h in (8, 12):
                        act.wait_ge(s_ao, b * 4 + (h // 4 - 1))
                    act.activation(OT[g32, h // 4, :], bank[6 + h % 2][0:32, :], ACT.Copy)
                    act.activation(sd[g32, h // 4 % 2, :], bank[6 + h % 2][32:64, :], ACT.Copy).then_inc(s_oe, 1)

                for h in range(HEADS):
                    act.wait_ge(s_mt, b * 16 + (h + 1))
                    act.activation(QS[96:128, h, :], bank[5][96:128, :].bitcast(F16)[:, 0:512], ACT.Copy).then_inc(s_mc, 1)
                    for t in range(TC):
                        act.wait_ge(s_st, b * 64 + (4 * h + t + 1))
                        if t == 0 and h >= 2:
                            act.wait_ge(s_av, b * 16 + (h - 1))
                        act.activation(PT[:, h % 2, t, :], bank[ST_BANK[(4 * h + t) % 3]][:, :], ACT.Exp,
                                       scale=float(DH) ** -0.5).then_inc(s_e, 1)
                    if h:
                        read_values(h - 1)
                    if h % 4 == 2 and h > 4:
                        attention_hi(h // 4 - 1)
                read_values(HEADS - 1)
                attention_hi(3)

            act.wait_ge(s_prep, 1)
            act.activation(HH[:, :, 0, :], v4(cT[:, :]), ACT.Copy).then_inc(s_h1, 1)
            groups(act, scan_group)
            act.wait_ge(s_np, T)
            act.activation(ng[:, :], npre[:, :], ACT.Tanh).then_inc(s_n, 1)
            act.wait_ge(s_zg, T)
            act.activation(zs[:, :], zg[:, :], ACT.Sigmoid).then_inc(s_z, 1)

        @block.vector
        def _(v):
            def evacuate_gi(g, gate, first):
                src = GI[gate]
                v.wait_ge(s_gim, g * 3 - 2 + gate)
                if gate == 0 and not first:
                    v.wait_ge(s_gic, g - 1)
                v.scalar_tensor_tensor(out=gie[:, gate % 2], in0=src[:, :, 1, :], scalar=1.0 / W_SCALE,
                                       in1=BIASB[:, 4 * gate:4 * gate + 4, :], op0=ALU.mult, op1=ALU.add).then_inc(s_gie, 1)
                v.wait_ge(s_gie, g * 3 - 2 + gate)
                v.scalar_tensor_tensor(out=GIn[:, 4 * gate:4 * gate + 4, :], in0=src[:, :, 0, :], scalar=1.0 / W_SCALE,
                                       in1=gie[:, gate % 2], op0=ALU.mult, op1=ALU.add).then_inc(s_gin, 1)

            def tanh_low(count):
                v.wait_ge(s_tf, count)
                v.tensor_tensor(TT[:, :, 1, :], v4(tf[:, :]), TT[:, :, 0, :], ALU.subtract).then_inc(s_t2, 1)

            def gru_n(m, t):
                v.wait_ge(s_rn, m + 1)
                v.tensor_tensor(v4(npre[:, :]), v4(rn[:, :]), GIc[:, 12:16, t * NB:(t + 1) * NB],
                                ALU.add).then_inc(s_np, 1)

            def scores(b):
                four = slice(b * TC, (b + 1) * TC)
                v.wait_ge(s_exp, (b + 1) * TC)
                v.reciprocal(rsum[:, four], esum[:, four]).then_inc(s_rs, 1)
                if b == 0:
                    v.wait_ge(s_par, 16 * 7)
                    v.wait_ge(s_tb, 16)
                v.wait_ge(s_rs, 2 * b + 1)
                v.scalar_tensor_tensor(out=rsc[:, four], in0=rsum[:, four], scalar=float(D) ** -0.5,
                                       in1=sideT[:, four], op0=ALU.mult, op1=ALU.mult).then_inc(s_rs, 1)
                v.wait_ge(s_rs, 2 * b + 2)
                for t in range(TC):
                    i = b * TC + t
                    v.scalar_tensor_tensor(out=ADJ[:, b, t, :], in0=ADJ[:, b, t, :], scalar=rsc[:, i:i + 1],
                                           in1=TB[:, b, :], op0=ALU.mult, op1=ALU.mult).then_inc(s_adj, 1)

            def cubic(count, c, q_s):
                v.wait_ge(s_sq, count)
                return v.scalar_tensor_tensor(out=ncub[:, :], in0=sq[:, :], scalar=c, in1=q_s,
                                              op0=ALU.subtract, op1=ALU.mult)

            def gru_z_half(m, t):
                v.wait_ge(s_ghz, m + 1)
                v.scalar_tensor_tensor(out=v4(zg1[:, :]), in0=GHZ[:, 1], scalar=1.0 / W_SCALE,
                                       in1=GIc[:, 8:12, t * NB:(t + 1) * NB], op0=ALU.mult, op1=ALU.add).then_inc(s_zg1, 1)

            def gru_z(m):
                v.wait_ge(s_zg1, m + 1)
                v.scalar_tensor_tensor(out=v4(zg[:, :]), in0=GHZ[:, 0], scalar=1.0 / W_SCALE,
                                       in1=v4(zg1[:, :]), op0=ALU.mult, op1=ALU.add).then_inc(s_zg, 1)

            def scan_group(g, rk, gi, gru, tail):
                for k in range(GB):
                    n = g * GB + k
                    m = n - LAG * GB
                    after = tail or (gru and k > 0)
                    static = isinstance(n, int)
                    pre = [n * PRE]

                    def done(ins):
                        ins.then_inc(s_pre, 1)
                        pre[0] = pre[0] + 1
                        return pre[0]

                    for s in range(4):
                        c = C_STAGE[s]
                        w = [wa, wa, wb, w4][s]
                        q_s = zc[:, 0:16] if s == 0 else qq[s]
                        p_s = zc[:, 16:32] if s == 0 else pp[s]
                        if (rk or (k == 0 and gi)) and s == 0:
                            if static and n == 0:
                                v.tensor_copy(zc[:, :], zz[0]).then_inc(s_clip, 1)
                            else:
                                v.wait_ge(s_qs, n * 4)
                                if not (static and n < 2):
                                    v.wait_ge(s_x2, n - 1)
                                v.tensor_scalar(zc[:, :], zz[0], -CLAMP, CLAMP, ALU.max, ALU.min).then_inc(s_clip, 1)
                        first, last = s == 0, s == 3
                        if rk and not first:
                            v.wait_ge(s_qs, n * 4 + s)
                        if rk and first:
                            tanh_low(n * 4 + 1)
                            v.wait_ge(s_dd, n + 1)
                            v.wait_ge(s_clip, n + 1)
                            w_done = done(v.scalar_tensor_tensor(out=wa[:, :], in0=dd[:, k % 2, :], scalar=0.5 * DT,
                                                                 in1=zc[:, :], op0=ALU.mult, op1=ALU.add))
                        if rk and s == 1:
                            v.tensor_tensor(e1[:, :], zz[1], zc[:, :], ALU.subtract)
                        if rk and s == 2:
                            v.scalar_tensor_tensor(out=e2[:, :], in0=zz[2], scalar=2.0, in1=e1[:, :],
                                                   op0=ALU.mult, op1=ALU.add)
                        if rk and last:
                            e_done = done(v.tensor_tensor(e3[:, :], zz[3], e2[:, :], ALU.add))
                            tanh_low(n * 4 + 4)
                            v.wait_ge(s_pre, e_done)
                            w_done = done(v.scalar_tensor_tensor(out=w4[:, :], in0=e3[:, :], scalar=1.0 / 3.0,
                                                                 in1=dd6[:, k % 2, :], op0=ALU.mult, op1=ALU.add))
                        if rk and (first or last):
                            done(cubic(n * 4 + (s + 1), c, q_s))
                        if gru and last:
                            v.wait_ge(s_ghnr, m + 1)
                            if k == 0:
                                v.wait_ge(s_gic, g - 1)
                            v.scalar_tensor_tensor(out=nr1[:, :].rearrange("p (n b) -> p n b", b=NB), in0=GHN[:, 1],
                                                   scalar=1.0 / W_SCALE, in1=GIc[:, 0:8, k * NB:(k + 1) * NB],
                                                   op0=ALU.mult, op1=ALU.add).then_inc(s_nr1, 1)
                        if rk:
                            if first or last:
                                v.wait_ge(s_pre, w_done)
                            v.scalar_tensor_tensor(out=gq[:, :], in0=p_s, scalar=-c, in1=w[:, 0:16],
                                                   op0=ALU.mult, op1=ALU.add)
                            h_done = done(v.scalar_tensor_tensor(out=gp[:, :], in0=p_s, scalar=-c * EPSILON * BETA,
                                                                 in1=w[:, 16:32], op0=ALU.mult, op1=ALU.add))
                        if rk and s in (1, 2):
                            tanh_low(n * 4 + (s + 1))
                        if gru and last:
                            v.wait_ge(s_nr1, m + 1)
                            v.scalar_tensor_tensor(out=nr[:, :].rearrange("p (n b) -> p n b", b=NB), in0=GHN[:, 0],
                                                   scalar=1.0 / W_SCALE, in1=nr1[:, :].rearrange("p (n b) -> p n b", b=NB),
                                                   op0=ALU.mult, op1=ALU.add).then_inc(s_nr, 1)
                        if after and first:
                            gru_n(m - 1, (k - 1) % GB)

                        def next_p():
                            v.scalar_tensor_tensor(out=pp[(s + 1) % 4], in0=q_s, scalar=c * EPSILON, in1=gp[:, :],
                                                   op0=ALU.mult, op1=ALU.add)

                        if rk:
                            v.wait_ge(s_pre, h_done)
                        if rk and s in (1, 2):
                            next_p()
                            v.wait_ge(s_pre, done(cubic(n * 4 + (s + 1), c, q_s)))
                        if rk:
                            b_done = done(v.tensor_tensor(base[:, :], gq[:, :], ncub[:, :], ALU.subtract))
                        if after and first:
                            gru_z_half(m - 1, (k - 1) % GB)
                        if rk and first:
                            v.scalar_tensor_tensor(out=wb[:, :], in0=dd[:, k % 2, :], scalar=DT,
                                                   in1=zc[:, :], op0=ALU.mult, op1=ALU.add)
                        if after and first:
                            gru_z(m - 1)
                        if rk and (first or last):
                            next_p()
                        if gi and (k, s) in EVACUATE:
                            evacuate_gi(g, EVACUATE.index((k, s)), not gru)
                        if rk:
                            v.wait_ge(s_cp, n * 4 + (s + 1))
                            v.wait_ge(s_pre, b_done)
                            u_done = done(v.scalar_tensor_tensor(out=v4(part[:, :]), in0=CPL[:, 1], scalar=c / W_SCALE,
                                                                 in1=v4(base[:, :]), op0=ALU.mult, op1=ALU.add))
                            v.wait_ge(s_pre, u_done)
                            v.scalar_tensor_tensor(out=v4(QP), in0=CPL[:, 0], scalar=c / W_SCALE,
                                                   in1=v4(part[:, :]), op0=ALU.mult, op1=ALU.add).then_inc(s_q, 1)
                            v.scalar_tensor_tensor(out=v4(qq[(s + 1) % 4]), in0=CPL[:, 0], scalar=c / W_SCALE,
                                                   in1=v4(part[:, :]), op0=ALU.mult, op1=ALU.add).then_inc(s_qs, 1)
                        if gru and s == 3:
                            v.wait_ge(s_r, m + 1)
                            v.tensor_tensor(rn[:, :], rg[:, :], nr[:, 0:16], ALU.mult).then_inc(s_rn, 1)

            for b in range(NB):
                v.wait_ge(sx[b], 16)
                for t in range(TC):
                    i = b * TC + t
                    v.reduce_max(nmx[:, i:i + 1], X[:, b, t, :], AX_X, negate=True).then_inc(s_max, 1)
                if b:
                    scores(b - 1)
            scores(NB - 1)
            v.wait_ge(s_emb, 1)
            for c in range(KC):
                v.tensor_scalar(mod_b[:, c, :], bank[4][:, (4 + c) * NB:(5 + c) * NB], bemb[:, 4 + c:5 + c], None, ALU.add)
                v.tensor_scalar(mod_a[:, c, :], bank[4][:, c * NB:(c + 1) * NB], bemb[:, c:c + 1], 1.0,
                                ALU.add, ALU.add).then_inc(s_modt, 1)
            v.wait_ge(s_modt, KC)
            for c in range(KC):
                v.tensor_scalar(mod_a[:, c, :], mod_a[:, c, :], gn[:, c:c + 1], None, ALU.mult)
            v.tensor_scalar(gqs[:, :], gqk[:, :], 1.0 / W_SCALE, None, ALU.mult)

            v.wait_ge(s_bits, 1)
            v.tensor_copy(biti[:, :], bitf[:, :])
            v.memset(zero[:, :], 0)
            v.memset(cand[:, :], 0).then_inc(s_cand, 1)

            def compare(e, pair):
                for j in range(2):
                    v.wait_ge(s_cand, 1)
                    if e:
                        v.wait_ge(s_mused, e * 2 + (j - 1))
                    b = 2 * pair + j
                    v.tensor_scalar(MASK[:, j, :], ADJ_B[:, b, :], candf[:, b:b + 1], None, ALU.is_ge).then_inc(s_mask, 1)

            v.wait_ge(s_diag, NT)
            compare(0, 0)
            compare(1, 1)
            for pair in range(2):
                two = slice(2 * pair, 2 * pair + 2)
                v.wait_ge(s_tot, pair + 1)
                v.tensor_scalar(key[:, two], bank[2 + pair][:, 0:2], TOPK - 0.5, -1.0, ALU.is_lt,
                                ALU.mult).then_inc(s_add, 1)
                v.wait_ge(s_add, pair + 1)
                v.scalar_tensor_tensor(out=cand[:, two], in0=zero[:, two], scalar=biti[:, 0:1], in1=key[:, two],
                                       op0=ALU.bitwise_or, op1=ALU.bitwise_xor).then_inc(s_cand, 1)

            def decide_bit(e, pair, d, bit):
                two = slice(2 * pair, 2 * pair + 2)
                if not (isinstance(d, int) and d < 4):
                    v.wait_ge(s_key, d - 3)
                v.wait_ge(s_tot, e + 1)
                v.tensor_scalar(addb[:, two], bank[2 + pair][:, 0:2], TOPK - 0.5, bitf[:, bass.ds(bit, 1)], ALU.is_ge,
                                ALU.mult).then_inc(s_add, 1)
                v.wait_ge(s_add, d + 1)
                v.scalar_tensor_tensor(out=cand[:, two], in0=addb[:, two], scalar=biti[:, bass.ds(bit + 1, 1)],
                                       in1=key[:, two], op0=ALU.bitwise_xor, op1=ALU.bitwise_xor).then_inc(s_cand, 1)

            def compare_next(e, pair, d, source, new_bit=True):
                two = slice(2 * pair, 2 * pair + 2)
                for j in range(2):
                    v.wait_ge(s_cand, d + 1)
                    v.wait_ge(s_mused, e * 2 + (j - 1))
                    v.tensor_scalar(MASK[:, j, :], source[:, 2 * pair + j, :], candf[:, 2 * pair + j:2 * pair + j + 1],
                                    None, ALU.is_ge).then_inc(s_mask, 1)
                    if j == 0 and new_bit:
                        v.tensor_tensor(key[:, two], key[:, two], addb[:, two], ALU.bitwise_xor).then_inc(s_key, 1)

            v.wait_ge(s_trunc, NT)
            compare_next(2, 0, 2, TRUNC, False)
            compare_next(3, 1, 2, TRUNC, False)
            decide_bit(2, 0, 2, 0)
            compare_next(4, 0, 3, TRUNC)
            decide_bit(3, 1, 3, 0)
            with v.Fori(0, 7) as i:
                for r in range(2):
                    compare_next(i * 4 + (5 + 2 * r), 1, i * 4 + (4 + 2 * r), TRUNC)
                    decide_bit(i * 4 + (4 + 2 * r), 0, i * 4 + (4 + 2 * r), i * 2 + (1 + r))
                    compare_next(i * 4 + (6 + 2 * r), 0, i * 4 + (5 + 2 * r), TRUNC)
                    decide_bit(i * 4 + (5 + 2 * r), 1, i * 4 + (5 + 2 * r), i * 2 + (1 + r))
            compare_next(33, 0, 32, ADJ_B, False)
            with v.Fori(0, 16) as i:
                compare_next(i * 2 + 34, 1, i * 2 + 32, ADJ_B)
                decide_bit(i * 2 + 33, 0, i * 2 + 32, i + 15)
                compare_next(i * 2 + 35, 0, i * 2 + 33, ADJ_B)
                decide_bit(i * 2 + 34, 1, i * 2 + 33, i + 15)
            v.wait_ge(s_cand, 65)
            for b in range(NB):
                for t in range(TC):
                    v.scalar_tensor_tensor(out=X[:, b, t, :], in0=ADJ[:, b, t, :], scalar=candf[:, b:b + 1],
                                           in1=X[:, b, t, :], op0=ALU.is_ge, op1=ALU.add).then_inc(s_x0, 1)
            v.wait_ge(s_x0, NT)
            v.memset(eps[:, :], 1e-6).then_inc(s_ye, 4)
            v.wait_ge(s_std, 1)
            v.reciprocal(rstd[:, :], stdx[:, :]).then_inc(s_rstd, 1)

            with v.Fori(0, NB) as b:
                for t in range(TC):
                    v.tensor_copy(XB[:, t, :], X[:, b, t, :]).then_inc(s_xb, 1)
                for c in range(KC):
                    v.wait_ge(s_xT, b * 4 + (c + 1))
                    if c >= 2:
                        v.wait_ge(s_xn, b * 4 + (c - 1))
                    v.tensor_scalar(xnf[:, c % 2, :], bank[3 + c % 2][:, :], mod_a[:, c, bass.ds(b, 1)],
                                    mod_b[:, c, bass.ds(b, 1)], ALU.mult, ALU.add).then_inc(s_xnf, 1)
                for cc in range(8):
                    v.wait_ge(s_sd, b * 8 + (cc + 1))
                    v.reciprocal(sd[:, cc % 2, :], sd[:, cc % 2, :]).then_inc(s_rr, 1)
                    v.wait_ge(s_rr, b * 8 + (cc + 1))
                    if cc >= 2:
                        v.wait_ge(s_ql, b * 8 + (cc - 1))
                    v.scalar_tensor_tensor(out=qn[:, cc % 2, :], in0=bank[PROJ_BANK[cc % 4]][:, :],
                                           scalar=gqs[:, cc % 2:cc % 2 + 1], in1=sd[:, cc % 2, :],
                                           op0=ALU.mult, op1=ALU.mult).then_inc(s_qn, 1)

                def row_max(h, t):
                    if h >= 2 and t == 0:
                        v.wait_ge(s_mt, b * 16 + (h - 1))
                    v.wait_ge(s_a, b * 64 + (4 * h + t + 1))
                    v.reduce_max(M16[:, h % 2, t, 0:1], bank[t % 2][:, :], AX_X).then_inc(s_mx, 1)

                def invert_sums(c, t):
                    if t == 0:
                        v.wait_ge(s_oe, b * 16 + (4 * c + 4))
                    part_c = sd[:, c % 2, t * P:(t + 1) * P]
                    v.reciprocal(part_c, part_c).then_inc(s_ri, 1)

                def normalise(c):
                    v.wait_ge(s_ri, b * 16 + (4 * c + 4))
                    v.tensor_tensor(OT[:, c, :], OT[:, c, :], sd[:, c % 2, :], ALU.mult).then_inc(s_ao, 1)

                for t in range(TC):
                    row_max(0, t)
                for h in range(HEADS + 2):
                    inverts = h % 4 == 1 and h > 1
                    for t in range(TC):
                        if h + 1 < HEADS:
                            row_max(h + 1, t)
                        if inverts:
                            invert_sums(h // 4 - 1, t)
                    if inverts:
                        normalise(h // 4 - 1)
                for n in range(KC + 1):
                    if n < KC:
                        v.wait_ge(s_y, b * 4 + (n + 1))
                        if n >= 2:
                            v.wait_ge(s_x1, b * 4 + (n - 1))
                        v.scalar_tensor_tensor(out=qn[:, n % 2, :], in0=bank[PROJ_BANK[n]][:, :], scalar=1.0 / W_SCALE,
                                               in1=OT[:, n, :], op0=ALU.mult, op1=ALU.add).then_inc(s_ye, 1)
                    if n:
                        v.wait_ge(s_ye, b * 4 + (4 + n))
                        v.tensor_tensor(X1V[:, n - 1, b, :], X1V[:, n - 1, b, :], qn[:, (n - 1) % 2, :],
                                        ALU.add).then_inc(s_x1, 1)

            v.memset(ones[:, :], 1.0).then_inc(s_ones, 1)
            v.wait_ge(s_ones, 1)
            for i in range(12):
                v.tensor_scalar(BIASB[:, i, :], ones[:, :], bg24[:, i:i + 1], bg24[:, 12 + i:13 + i] if i < 8 else None,
                                ALU.mult, ALU.add if i < 8 else ALU.bypass)
            for i in range(4):
                v.tensor_scalar(GIc[:, i, :], ones[:, :], bg24[:, 20 + i:21 + i], None, ALU.mult)
            for u in range(2):
                v.memset(dd[:, u, 16:32], EPSILON * ALPHA)
            v.memset(dt6[:, :], DT / 6.0)
            v.memset(X1F[:, T], 0.0)
            v.tensor_copy(zz[0][:, 0:16], cT[:, :])
            v.tensor_copy(zz[0][:, 16:32], cT[:, :])
            v.tensor_copy(hst[:, :], cT[:, :]).then_inc(s_prep, 1)
            v.wait_ge(s_prep, 1)
            v.tensor_copy(QP, cT[:, :]).then_inc(s_q, 1)
            groups(v, scan_group)
            gru_n(T - 1, GB - 1)
            gru_z_half(T - 1, GB - 1)
            gru_z(T - 1)

        @block.gpsimd
        def _(pool):
            def update_h(m):
                pool.wait_ge(s_n, m + 1)
                pool.tensor_tensor(hd[:, :], hst[:, :], ng[:, :], ALU.subtract).then_inc(s_hd, 1)
                pool.wait_ge(s_z, m + 1)
                pool.wait_ge(s_hd, m + 1)
                pool.tensor_tensor(zd[:, :], zs[:, :], hd[:, :], ALU.mult).then_inc(s_zd, 1)
                pool.wait_ge(s_zd, m + 1)
                pool.tensor_tensor(hst[:, :], ng[:, :], zd[:, :], ALU.add).then_inc(s_h, 1)

            def add_h(m):
                pool.wait_ge(s_h, m + 2)
                pool.tensor_tensor(X1F[:, m], X1F[:, m], hst[:, :], ALU.add).then_inc(s_o, 1)

            def sum_drive(n, u):
                pool.tensor_tensor(dd[:, u, 0:16], X1F[:, n], bl2[:, :], ALU.add).then_inc(s_dsum, 1)

            def scale_drive(n, u):
                pool.wait_ge(s_dsum, n + 1)
                pool.tensor_tensor(dd6[:, u, :], dd[:, u, :], dt6[:, :], ALU.mult).then_inc(s_dd, 1)

            def scan_group(g, rk, gi, gru, tail):
                for k in range(GB):
                    n = g * GB + k
                    m = n - LAG * GB
                    after = tail or (gru and k > 0)
                    static = isinstance(n, int)
                    if after:
                        update_h(m - 1)
                        pool.wait_ge(s_h1, m + 1)
                        pool.tensor_tensor(HH[:, :, 1, :], v4(hst[:, :]), HH[:, :, 0, :], ALU.subtract).then_inc(s_h2, 1)
                    x2 = (rk or (k == 0 and gi)) and not (static and n == 0)
                    t = (k - 1) % GB
                    if x2 and not (static and n == 1):
                        pool.wait_ge(s_xl, n - 1)
                    if x2 and k == 1 and not (static and g == 0):
                        pool.wait_ge(s_xg, g)
                    if rk or x2:
                        pool.wait_ge(s_clip, n + 1)
                    if rk:
                        sum_drive(n + 1, (k + 1) % 2)
                    if x2:
                        pool.tensor_tensor(x2f[:, :], X1F[:, n - 1], zc[:, 0:16], ALU.add).then_inc(s_xf, 1)
                        pool.tensor_tensor(XGn[:, :, 0, t, :], v4(X1F[:, n - 1]), v4(zc[:, 0:16]),
                                           ALU.add).then_inc(s_xh, 1)
                    if rk:
                        scale_drive(n + 1, (k + 1) % 2)
                    if x2:
                        pool.wait_ge(s_xf, n)
                        pool.wait_ge(s_xh, n)
                        pool.tensor_tensor(XGn[:, :, 1, t, :], v4(x2f[:, :]), XGn[:, :, 0, t, :],
                                           ALU.subtract).then_inc(s_xl, 1)
                        pool.tensor_tensor(X1F[:, n - 1], X1F[:, n - 1], zc[:, 0:16], ALU.add).then_inc(s_x2, 1)
                        if k == 0:
                            pool.wait_ge(s_xl, n)
                            if not (static and g == 1):
                                pool.wait_ge(s_gim, g * 3 - 3)
                            pool.tensor_tensor(XGc[:, :, :, :, :].rearrange("p c h t b -> p (c h t b)"),
                                               XGn[:, :, :, :, :].rearrange("p c h t b -> p (c h t b)"), ones16[:, :],
                                               ALU.mult).then_inc(s_xg, 1)
                    if after:
                        add_h(m - 1)

            for a in (identf, blk32):
                pool.memset(a[:, :], 0.0 if a is identf else 1.0)
            pool.memset(ones16[:, :], 1.0)
            pool.memset(W_SCALES, W_SCALE)
            pool.memset(M16[:, :, :, :], 0.0)
            for j in range(31):
                pool.memset(bitf[:, j:j + 1], float(2 ** (30 - j)))
            pool.memset(bitf[:, 31:32], 0.0).then_inc(s_bits, 1)
            pool.wait_ge(s_bits, 1)
            pool.affine_select(out=identf[:, :], in_=identf[:, :], compare_op=ALU.not_equal, fill=1.0, base=0,
                               pattern=[[-1, P]], channel_multiplier=1).then_inc(s_iota, 1)
            pool.affine_select(out=blk32[:, :], in_=blk32[:, :], compare_op=ALU.is_ge, fill=0.0, base=0,
                               pattern=[[-32, 4], [0, 32]], channel_multiplier=1).then_inc(s_iota, 1)
            pool.wait_ge(s_iota, 2)
            pool.affine_select(out=blk32[:, :], in_=blk32[:, :], compare_op=ALU.is_ge, fill=0.0, base=31,
                               pattern=[[32, 4], [0, 32]], channel_multiplier=-1)
            pool.tensor_copy(ident16[:, :], identf[:, :]).then_inc(s_const, 1)
            for i in range(NT):
                b, t = i // TC, i % TC
                pool.wait_ge(s_adj, i + 1)
                a = ADJ[:, b, t, t * P:(t + 1) * P]
                pool.affine_select(out=a, in_=a, compare_op=ALU.not_equal, fill=DIAGONAL, base=0,
                                   pattern=[[-1, P]], channel_multiplier=1).then_inc(s_diag, 1)
            with pool.Fori(0, PIECES // 2) as i:
                for u in range(2):
                    pool.wait_ge(s_whi, i * 2 + (u + 1))
                    pool.tensor_tensor(STG[:, u, :], STG[:, u, :], W_SCALES, ALU.mult).then_inc(s_wsc, 1)
                    pool.wait_ge(s_wsc, i * 2 + (u + 1))
                    pool.tensor_tensor(HALF[:, u, 1, :], STG[:, u, :], HALF[:, u, 0, :], ALU.subtract).then_inc(s_wlo, 1)
            pool.wait_ge(s_wlo, PIECES)
            pool.wait_ge(s_x0, NT)
            pool.memset(KS[96:128, :, :], -1.0).then_inc(s_kv, 1)
            pool.wait_ge(s_kv, 1)
            pool.memset(V[:, :, :, DH:2 * DH], 1.0).then_inc(s_kv, 1)

            with pool.Fori(0, NB) as b:
                for c in range(KC):
                    pool.wait_ge(s_xnh, b * 4 + (c + 1))
                    pool.tensor_tensor(XN[:, 1, c, :], xnf[:, c % 2, :], XN[:, 0, c, :], ALU.subtract).then_inc(s_xn, 1)
                for cc in range(8):
                    pool.wait_ge(s_qh, b * 8 + (cc + 1))
                    if cc >= 2:
                        pool.wait_ge(s_qst[cc % 2], b * 128 + (cc // 2) * 32)
                    pool.tensor_tensor(QKH[:, cc % 2, 1, :], qn[:, cc % 2, :], QKH[:, cc % 2, 0, :],
                                       ALU.subtract).then_inc(s_ql, 1)
                for c in range(KC):
                    pool.wait_ge(s_oh, b * 4 + (c + 1))
                    pool.tensor_tensor(OTH[:, 1, c, :], OT[:, c, :], OTH[:, 0, c, :], ALU.subtract).then_inc(s_ol, 1)

            pool.wait_ge(s_prep, 1)
            pool.wait_ge(s_x1, 16)
            pool.wait_ge(s_h1, 1)
            pool.tensor_tensor(HH[:, :, 1, :], v4(hst[:, :]), HH[:, :, 0, :], ALU.subtract).then_inc(s_h2, 1)
            pool.tensor_copy(hd[:, :], hst[:, :]).then_inc(s_h, 1)
            sum_drive(0, 0)
            scale_drive(0, 0)
            groups(pool, scan_group)
            update_h(T - 1)
            add_h(T - 1)

        @block.sync
        def _(sp):
            for b in range(NB):
                sp.dma_start(X[:, b], x[b].rearrange("(t p) d -> p t d", p=P)).then_inc(sx[b], 16)
                if b == 0:
                    sp.dma_start(sideT[:, :], side).then_inc(s_par, 16)
                    sp.dma_start(cT[:, :], condT).then_inc(s_par, 16)
                    sp.dma_start(bemb[:, :], b_emb).then_inc(s_par, 16)
                    sp.dma_start(gn[:, :], g_norm).then_inc(s_par, 16)
                    sp.dma_start(gqk[:, :], g_qk).then_inc(s_par, 16)
                    sp.dma_start(bl2[:, :], bias_l2).then_inc(s_par, 16)
                    sp.dma_start(bg24[:, :], b_gates).then_inc(s_par, 16)
                    sp.dma_start(TB, cond.partition_broadcast(P)).then_inc(s_tb, 16)
            sp.dma_start(WE, W_emb.rearrange("(k p) n -> p k n", p=P)).then_inc(s_we, 16)

            def load_piece(i, u):
                sp.dma_start(STG[:, u, :], W_all[:, bass.ds((i * 2 + u) * W_PIECE, W_PIECE)]).then_inc(s_wld[u], 16)

            def store_piece(i, u):
                sp.wait_ge(s_wlo, i * 2 + (u + 1))
                sp.dma_start(W16F[:, :, bass.ds((i * 2 + u) * W_PIECE, W_PIECE)], HALF[:, u]).then_inc(s_wst[u], 16)

            for u in range(2):
                load_piece(0, u)
            with sp.Fori(0, PIECES // 2 - 1) as i:
                for u in range(2):
                    store_piece(i, u)
                    load_piece(i + 1, u)
            for u in range(2):
                store_piece(PIECES // 2 - 1, u)
            for u in range(2):
                sp.wait_ge(s_wst[u], 16 * PIECES // 2)
            sp.dma_start(W_Q[:, :, :, :], W16[:, :, :, C_QKV:C_OUT]).then_inc(s_wq, 16)
            sp.dma_start(W_O[:, :, :, :], W16[:, :, :, C_OUT:C_IH]).then_inc(s_wq, 16)

            with sp.Fori(0, NB) as b:
                for cc in range(9):
                    if cc < 8:
                        for half in range(2):
                            sp.wait_ge((s_qh, s_ql)[half], b * 8 + (cc + 1))
                            sp.dma_start(QKD[cc, half], QKH[:, cc % 2, half, :]).then_inc(s_qst[cc % 2], 16)
                    if cc:
                        lc = cc - 1
                        sp.wait_ge(s_qst[lc % 2], b * 128 + (lc // 2 * 32 + 32))
                        for r, half in enumerate(((0, 1, 0), (0, 0, 1))[lc % 2]):
                            sp.dma_start((QS, KS)[lc % 2][32 * r:32 * r + 32, 4 * (lc // 2):4 * (lc // 2) + 4, :],
                                         QKD[lc, half].rearrange("(g p) n -> p g n", g=4)).then_inc(s_qks[lc], 16)

            sp.wait_ge(s_xhat, NT)
            sp.wait_ge(s_xb, NT)
            sp.dma_start(W_CP, W16[:, :, :, C_CPL:C_ALL]).then_inc(s_wl, 16)
            sp.dma_start(W_HH, W16[:, :, :, C_HH:C_CPL]).then_inc(s_wl, 16)
            sp.wait_ge(s_av, NB * HEADS)
            sp.dma_start(W_IH, W16[:, :, :, C_IH:C_HH]).then_inc(s_wl, 16)
            with sp.Fori(0, NG) as j:
                sp.wait_ge(s_o, j * GB + GB)
                sp.dma_start(out[:, bass.ds(j * GB, GB), :], X1F[:, bass.ds(j * GB, GB), :]).then_inc(s_out, 16)
            sp.wait_ge(s_out, 16 * NG)


_ORDER = ["x", "side", "condT", "cond", "W_emb", "b_emb", "g_norm", "g_qk", "W_all", "bias_l2", "b_gates"]


def kernel(x, fside_BxSx1_0, cond_2048, L1_cond_W_emb, L1_cond_b_emb, L1_cond_g_norm, L1_cond_W_qkv, L1_cond_g_q,
           L1_cond_g_k, L1_cond_W_out, L2_cond_coupling, L2_cond_bias, L3_cond_W_ih, L3_cond_W_hh, L3_cond_b_ih,
           L3_cond_b_hh):
    import numpy as np
    import concourse.bacc as bacc
    from concourse.bass_utils import run_bass_kernel_spmd

    def columns(a):
        return np.asarray(a).reshape(-1, P).T

    cond = np.asarray(cond_2048)
    w_all = np.concatenate([np.asarray(L1_cond_W_qkv), np.asarray(L1_cond_W_out), np.asarray(L3_cond_W_ih),
                            np.asarray(L3_cond_W_hh), np.asarray(L2_cond_coupling).T], axis=1)
    arrays = {
        "x": np.asarray(x),
        "side": np.asarray(fside_BxSx1_0).reshape(NB * TC, P).T,
        "condT": cond.reshape(NB, KC, P).transpose(2, 1, 0).reshape(P, S16),
        "cond": cond,
        "W_emb": np.asarray(L1_cond_W_emb),
        "b_emb": columns(L1_cond_b_emb),
        "g_norm": columns(L1_cond_g_norm),
        "g_qk": np.stack([np.tile(np.asarray(L1_cond_g_q), P // DH), np.tile(np.asarray(L1_cond_g_k), P // DH)], axis=1),
        "W_all": w_all.reshape(KC, P, C_ALL).transpose(1, 0, 2).reshape(P, KC * C_ALL),
        "bias_l2": np.repeat(columns(L2_cond_bias), NB, axis=1),
        "b_gates": np.concatenate([columns(L3_cond_b_ih), columns(L3_cond_b_hh)], axis=1),
    }
    arrays = {k: np.ascontiguousarray(a) for k, a in arrays.items()}
    nc = bacc.Bacc("TRN2", target_bir_lowering=False, num_devices=1)
    args = [nc.dram_tensor(f"in_{k}", arrays[k].shape, mybir.dt.from_np(arrays[k].dtype), kind="ExternalInput").ap()
            for k in _ORDER]
    out = nc.dram_tensor("out_x", (P, T, S16), F32, kind="ExternalOutput").ap()
    mixed_scan_kernel(nc, *args, out)
    r = run_bass_kernel_spmd(nc, [{f"in_{k}": a for k, a in arrays.items()}], core_ids=[0])
    got = np.asarray(r.results[0]["out_x"]).reshape(P, T, KC, NB)
    return np.ascontiguousarray(got.transpose(3, 1, 2, 0).reshape(NB, T, D))
```
